# Optimizing a Trainium2 kernel written in Bass

```python
import numpy as np
import jax
import jax.numpy as jnp

def _softmax(x, axis=-1):
    return jax.nn.softmax(x, axis=axis)

def _gelu(x):
    return jax.nn.gelu(x, approximate=True)

def _silu(x):
    return jax.nn.silu(x)

def _sigmoid(x):
    return jax.nn.sigmoid(x)

def _layernorm(x, axis=-1, eps=1e-05):
    m = jnp.mean(x, axis=axis, keepdims=True)
    v = jnp.var(x, axis=axis, keepdims=True)
    return (x - m) / jnp.sqrt(v + eps)

def _scatter_add(tgt, idx, src, axis=0):
    return tgt.at[idx].add(src)

def _segment_sum(src, seg, n):
    return jax.ops.segment_sum(src, seg, n)
kernel_name = 'mk_adj_preln_d2_adj_r2_54a78e'

def setup_inputs(seed: int=0):
    np.random.seed(seed)
    _w = jnp.asarray

    def _rec_inputs():
        import jax
        import jax.numpy as jnp
        _gk = jax.random.key(seed)
        x = -0.0003929 + 0.9999 * jax.random.normal(jax.random.fold_in(_gk, 1), (8, 1024, 256), jnp.float32)
        _a = jax.random.bernoulli(jax.random.fold_in(_gk, 2), 0.00195312, (8, 1024, 1024))
        _a = jnp.logical_or(_a, jnp.eye(1024, dtype=bool))
        _af = _a.astype(jnp.float32)
        _af = _af * jax.random.uniform(jax.random.fold_in(_gk, 3), (8, 1024, 1024), jnp.float32, 0.05, 1)
        adj = _af
        return (x, adj)
    x, adj = _rec_inputs()

    def _L0_gnn_setup():
        import jax, jax.numpy as jnp
        import numpy as np
        EPS = 1e-06
        key = jax.random.key(seed)
        k1, k2, k3 = jax.random.split(key, 3)
        B, N, F, O = (8, 2048, 256, 256)
        x = jax.random.normal(k1, (B, N, F), dtype=jnp.float32)
        adj = jax.random.uniform(k2, (B, N, N), dtype=jnp.float32)
        W = jax.random.normal(k3, (O, 2 * F), dtype=jnp.float32) * (1.0 / np.sqrt(2 * F))
        return {'x': x, 'adj': adj, 'W': W}
    _L0_gnn_all = _L0_gnn_setup()
    _L0_gnn_in = {k: v for k, v in _L0_gnn_all.items() if k in ('W',)}
    del _L0_gnn_all

    def _L1_gnn_setup():
        import jax, jax.numpy as jnp
        import numpy as np
        EPS_LN = 1e-05

        def hypergraph_conv(x, adj, W, b):
            N, C, _ = adj.shape
            H = (adj != 0).astype(x.dtype)
            w = adj.reshape(N, -1)[:, :C]
            xw = jnp.einsum('ncd,hd->nch', x, W)
            Dn = jnp.einsum('nce,ne->nc', H, w)
            Dn = jnp.where(Dn > 0, 1.0 / Dn, 0.0)
            Be = H.sum(axis=1)
            Be = jnp.where(Be > 0, 1.0 / Be, 0.0)
            m = Be[:, :, None] * jnp.einsum('nce,nch->neh', H, xw)
            out = Dn[:, :, None] * jnp.einsum('nce,neh->nch', H, m)
            return out + b

        def layer_norm(x, g, b):
            mu = jnp.mean(x, axis=-1, keepdims=True)
            var = jnp.var(x, axis=-1, keepdims=True)
            return (x - mu) * jax.lax.rsqrt(var + EPS_LN) * g + b
        key = jax.random.key(seed)
        ks = jax.random.split(key, 4)
        N, C, Din, Dh, Dout = (16, 512, 256, 512, 256)
        x = jax.random.normal(ks[0], (N, C, Din), dtype=jnp.float32)
        adj = jax.random.uniform(ks[1], (N, C, C), dtype=jnp.float32, minval=0.1, maxval=1.0)
        W1 = jax.random.normal(ks[2], (Dh, Din), dtype=jnp.float32) * (1.0 / np.sqrt(Din))
        b1 = jnp.zeros((Dh,), dtype=jnp.float32)
        gamma = jnp.ones((Dh,), dtype=jnp.float32)
        beta = jnp.zeros((Dh,), dtype=jnp.float32)
        W2 = jax.random.normal(ks[3], (Dout, Dh), dtype=jnp.float32) * (1.0 / np.sqrt(Dh))
        b2 = jnp.zeros((Dout,), dtype=jnp.float32)
        return {'x': x, 'adj': adj, 'W1': W1, 'b1': b1, 'gamma': gamma, 'beta': beta, 'W2': W2, 'b2': b2}
    _L1_gnn_all = _L1_gnn_setup()
    _L1_gnn_in = {k: v for k, v in _L1_gnn_all.items() if k in ('W1', 'b1', 'gamma', 'beta', 'W2', 'b2')}
    del _L1_gnn_all
    return {'x': x, 'adj': adj, 'L0_gnn_W': _L0_gnn_in['W'], 'L1_gnn_W1': _L1_gnn_in['W1'], 'L1_gnn_b1': _L1_gnn_in['b1'], 'L1_gnn_gamma': _L1_gnn_in['gamma'], 'L1_gnn_beta': _L1_gnn_in['beta'], 'L1_gnn_W2': _L1_gnn_in['W2'], 'L1_gnn_b2': _L1_gnn_in['b2']}

def reference(x, adj, L0_gnn_W, L1_gnn_W1, L1_gnn_b1, L1_gnn_gamma, L1_gnn_beta, L1_gnn_W2, L1_gnn_b2):
    import jax
    import jax.numpy as jnp

    def _L0_gnn_ref(x, adj, W):
        import jax, jax.numpy as jnp
        import numpy as np
        EPS = 1e-06
        deg = jnp.sum(adj, axis=-1, keepdims=True)
        agg = jnp.einsum('bij,bjf->bif', adj, x) / jnp.maximum(deg, EPS)
        cat = jnp.concatenate([x, agg], axis=2)
        out = jnp.einsum('bnf,of->bno', cat, W)
        return jax.nn.relu(out)

    def _L1_gnn_ref(x, adj, W1, b1, gamma, beta, W2, b2):
        import jax, jax.numpy as jnp
        import numpy as np
        EPS_LN = 1e-05

        def hypergraph_conv(x, adj, W, b):
            N, C, _ = adj.shape
            H = (adj != 0).astype(x.dtype)
            w = adj.reshape(N, -1)[:, :C]
            xw = jnp.einsum('ncd,hd->nch', x, W)
            Dn = jnp.einsum('nce,ne->nc', H, w)
            Dn = jnp.where(Dn > 0, 1.0 / Dn, 0.0)
            Be = H.sum(axis=1)
            Be = jnp.where(Be > 0, 1.0 / Be, 0.0)
            m = Be[:, :, None] * jnp.einsum('nce,nch->neh', H, xw)
            out = Dn[:, :, None] * jnp.einsum('nce,neh->nch', H, m)
            return out + b

        def layer_norm(x, g, b):
            mu = jnp.mean(x, axis=-1, keepdims=True)
            var = jnp.var(x, axis=-1, keepdims=True)
            return (x - mu) * jax.lax.rsqrt(var + EPS_LN) * g + b
        h = jax.nn.relu(hypergraph_conv(x, adj, W1, b1))
        h = layer_norm(h, gamma, beta)
        y = hypergraph_conv(h, adj, W2, b2)
        return y + x
    h = jnp.maximum(_layernorm(x, axis=-1), 0.0)
    x = x + _L0_gnn_ref(h, adj, L0_gnn_W)
    h = jnp.maximum(_layernorm(x, axis=-1), 0.0)
    x = x + _L1_gnn_ref(h, adj, L1_gnn_W1, L1_gnn_b1, L1_gnn_gamma, L1_gnn_beta, L1_gnn_W2, L1_gnn_b2)
    return x

_drawn_inputs = setup_inputs


def setup_inputs(seed=0):
    import zlib

    import numpy as np

    out = dict(_drawn_inputs(seed))
    spreads = {'L1_gnn_b1': (0.0, 0.1),
     'L1_gnn_gamma': (1.0, 0.2),
     'L1_gnn_beta': (0.0, 0.1),
     'L1_gnn_b2': (0.0, 0.1)}
    factors = {}
    for name, (base, spread) in spreads.items():
        noise = np.random.default_rng([zlib.crc32(name.encode()), seed]).standard_normal(out[name].shape)
        drawn = base * np.exp(spread * noise) if base else spread * noise
        out[name] = jnp.asarray(drawn.astype(out[name].dtype))
    for name, factor in factors.items():
        out[name] = (out[name] * factor).astype(out[name].dtype)
    return out
```

```python
from contextlib import ExitStack

import concourse.bass as bass
from concourse import mybir
from concourse.alu_op_type import AluOpType as ALU


F32 = mybir.dt.float32
F32R = mybir.dt.float32r
ACT = mybir.ActivationFunctionType

P = 128
ACC_BANKS = 6
TP_BANKS = 2
SLOTS = 4
DEG_EPS = 1e-6
LN_EPS = 1e-5
TINY = 1.1754944e-38
DMA = 16


def acc_order(NT, chunks, FT):
    order = [("Z", i) for i in range(NT)] + [("A", i) for i in range(NT)] + [("C1", i) for i in range(NT)]
    order += [("C2", c * FT + f) for c in range(chunks) for f in range(FT)]
    for i in range(NT + 3):
        if i < NT:
            order.append(("W1", i))
        if i >= 3:
            order.append(("W2", i - 3))
    order += [("C3", i) for i in range(NT)] + [("C4", i) for i in range(NT)]
    return {key: n for n, key in enumerate(order)}


def build(nc, x, adj, adj_t, w0, w1, w2, b1, b2, gamma, beta, ident, out):
    B, N, _ = adj.shape
    F = x.shape[2]
    D = w1.shape[2]
    NT = N // P
    FT = F // P
    DT = D // P
    CH = N // 512
    FP = F + 2
    NUM = acc_order(NT, CH, FT)
    PER = len(NUM)
    TPS = 2 * NT
    assert PER % ACC_BANKS == 0 and TPS % TP_BANKS == 0 and NT % SLOTS == 0 and D == 512

    with ExitStack() as ctx:
        def sb(name, shape, dt=F32):
            return ctx.enter_context(nc.sbuf_tensor(name, shape, dt))

        def sem(name):
            return ctx.enter_context(nc.semaphore(name))

        adj_in = sb("adj_in", [P, SLOTS, N])
        adjT_in = sb("adjT_in", [P, SLOTS, NT, P])
        H = sb("H", [P, NT, N], F32R)
        HT = sb("HT", [P, NT, N], F32R)
        x_sb = sb("x_sb", [P, NT, F])
        s_sb = sb("s_sb", [P, NT, F])
        fbuf = sb("fbuf", [P, NT * F])
        zb = sb("zb", [P, NT, F + 1])
        v_hi = sb("v_hi", [P, NT, FP], F32R)
        v_lo = sb("v_lo", [P, NT, F], F32R)
        g_hi = sb("g_hi", [P, NT, F], F32R)
        g_lo = sb("g_lo", [P, NT, F], F32R)
        w0_sb = sb("w0_sb", [P, FT, 2 * F])
        w1_sb = sb("w1_sb", [P, FT, D])
        w2_sb = sb("w2_sb", [P, DT, F])
        b1_sb = sb("b1_sb", [P, D])
        b2_sb = sb("b2_sb", [P, F])
        gamma_sb = sb("gamma_sb", [P, DT])
        beta_sb = sb("beta_sb", [P, DT])
        ident_sb = sb("ident_sb", [P, P])
        wrow = sb("wrow", [P, N])
        h0 = sb("h0", [P, 3, F])
        u_sb = sb("u_sb", [P, 2, F])
        h_sb = sb("h_sb", [P, 2, F])
        v1_sb = sb("v1_sb", [P, D])
        t_sb = sb("t_sb", [P, 3, D])
        hnT = sb("hnT", [P, 2, DT, P])
        neg_half = sb("neg_half", [P, 1])
        zero = sb("zero", [P, 1])
        eps = sb("eps", [P, 1])
        neg_mean = sb("neg_mean", [P, 2, NT])
        x_st = sb("x_st", [P, NT, 6])
        x_mv = sb("x_mv", [P, NT, 2])
        x1_st = sb("x1_st", [P, NT, 6])
        x1_mv = sb("x1_mv", [P, NT, 2])
        t_st = sb("t_st", [P, NT, 6])
        t_mv = sb("t_mv", [P, NT, 2])
        ve = sb("ve", [P, 3, NT])
        rstd = sb("rstd", [P, 3, NT])
        nmr = sb("nmr", [P, 2, NT])
        deg = sb("deg", [P, NT])
        deg_inv = sb("deg_inv", [P, NT])
        cnt = sb("cnt", [P, NT])
        b_inv = sb("b_inv", [P, NT])
        d_sum = sb("d_sum", [P, NT])
        d_pos = sb("d_pos", [P, NT])
        d_safe = sb("d_safe", [P, NT])
        d_rec = sb("d_rec", [P, NT])
        d_inv = sb("d_inv", [P, NT])

        h0T = fbuf[:, :].rearrange("p (i f n) -> p i f n", i=NT, f=FT)
        za = fbuf[:, :].rearrange("p (i f) -> p i f", i=NT)
        uT = fbuf[:, :].rearrange("p (f n) -> p f n", f=FT)

        acc_banks = [ctx.enter_context(nc.psum_tensor(f"acc{k}", [P, 512], F32)) for k in range(ACC_BANKS)]
        tp_banks = [ctx.enter_context(nc.psum_tensor(f"tp{k}", [P, 512], F32)) for k in range(TP_BANKS)]

        def acc(key, i):
            return acc_banks[NUM[key, i] % ACC_BANKS]

        adj_loaded = [sem(f"adj_loaded{k}") for k in range(SLOTS)]
        adjT_loaded = [sem(f"adjT_loaded{k}") for k in range(SLOTS)]
        x_loaded = sem("x_loaded")
        wrow_loaded = sem("wrow_loaded")
        ident_loaded = sem("ident_loaded")
        w0_loaded = sem("w0_loaded")
        rest_loaded = sem("rest_loaded")
        out_stored = sem("out_stored")
        acc_full = sem("acc_full")
        acc_drained = sem("acc_drained")
        tp_full = sem("tp_full")
        tp_drained = sem("tp_drained")
        ones_set = sem("ones_set")
        consts_set = sem("consts_set")
        x_stats = sem("x_stats")
        x_moments = sem("x_moments")
        x_ve = sem("x_ve")
        x_rstd = sem("x_rstd")
        x_ln = sem("x_ln")
        h0_ready = sem("h0_ready")
        H_set = sem("H_set")
        adj_used = sem("adj_used")
        d_positive = sem("d_positive")
        d_guarded = sem("d_guarded")
        d_divided = sem("d_divided")
        d_ready = sem("d_ready")
        za_ready = sem("za_ready")
        deg_guarded = sem("deg_guarded")
        deg_divided = sem("deg_divided")
        x1_ready = sem("x1_ready")
        x1_stats = sem("x1_stats")
        x1_moments = sem("x1_moments")
        x1_ve = sem("x1_ve")
        x1_rstd = sem("x1_rstd")
        x1_ln = sem("x1_ln")
        h_ready = sem("h_ready")
        h_split = sem("h_split")
        s_biased = sem("s_biased")
        s_ready = sem("s_ready")
        adjT_used = sem("adjT_used")
        cnt_guarded = sem("cnt_guarded")
        b_ready = sem("b_ready")
        g_hi_ready = sem("g_hi_ready")
        t_ready = sem("t_ready")
        t_stats = sem("t_stats")
        t_moments = sem("t_moments")
        t_ve = sem("t_ve")
        t_rstd = sem("t_rstd")
        n_ready = sem("n_ready")
        y_hi_ready = sem("y_hi_ready")

        def tile(b, i):
            return b * NT + (i + 1)

        def full(b, key, i):
            return b * PER + (NUM[key, i] + 1)

        def drained(b, key, i):
            return b * PER + (NUM[key, i] + 1 + ACC_BANKS)

        def bank_free(b, key, i):
            return b * PER + (NUM[key, i] + 1)

        def hn_group(b, i):
            return b * TPS + (NT + i)

        def h0_group(b, i):
            return b * TPS + i

        def loaded(b, i):
            return b * (DMA * NT // SLOTS) + DMA * (i // SLOTS + 1)

        block = ctx.enter_context(nc.Block())

        @block.sync
        def _(sp):
            def load_adj(b, i):
                sp.dma_start(adj_in[:, i % SLOTS, :], adj[b, i * P:(i + 1) * P, :]).then_inc(adj_loaded[i % SLOTS], DMA)

            def load_adjT(b, i):
                sp.dma_start(adjT_in[:, i % SLOTS, :, :], adj_t[b, i]).then_inc(adjT_loaded[i % SLOTS], DMA)

            def load_x(b):
                sp.dma_start(x_sb[:, :, :], x[b].rearrange("(i p) f -> p i f", p=P)).then_inc(x_loaded, DMA)

            def load_wrow(b):
                sp.dma_start(wrow[:, :], adj[b, 0:1, :].to_broadcast([P, N])).then_inc(wrow_loaded, DMA)

            sp.sem_inc(out_stored, DMA)
            load_x(0)
            sp.dma_start(ident_sb[:, :], ident).then_inc(ident_loaded, DMA)
            sp.dma_start(w0_sb[:, :, :], w0).then_inc(w0_loaded, DMA)
            load_wrow(0)
            for i in range(SLOTS):
                load_adjT(0, i)
                load_adj(0, i)
            for dst, src in ((w1_sb, w1), (w2_sb, w2)):
                sp.dma_start(dst[:, :, :], src).then_inc(rest_loaded, DMA)
            for dst, src in ((b1_sb, b1), (b2_sb, b2), (gamma_sb, gamma), (beta_sb, beta)):
                sp.dma_start(dst[:, :], src).then_inc(rest_loaded, DMA)

            def graph(b, more):
                for i in range(SLOTS, NT):
                    sp.wait_ge(adj_used, tile(b, i - SLOTS))
                    load_adj(b, i)
                for i in range(SLOTS, NT):
                    sp.wait_ge(adjT_used, tile(b, i - SLOTS))
                    load_adjT(b, i)
                if more:
                    for i in range(SLOTS):
                        sp.wait_ge(adj_used, tile(b, NT - SLOTS + i))
                        load_adj(b + 1, i)
                    load_wrow(b + 1)
                    for i in range(SLOTS):
                        sp.wait_ge(adjT_used, tile(b, NT - SLOTS + i))
                        load_adjT(b + 1, i)
                    sp.wait_ge(x1_ready, tile(b, NT - 1))
                    load_x(b + 1)
                for i in range(NT):
                    sp.wait_ge(acc_drained, drained(b, "C4", i))
                    sp.dma_start(out[b, i * P:(i + 1) * P, :], s_sb[:, i, :]).then_inc(out_stored, DMA)

            with sp.Fori(0, B - 1) as b:
                graph(b, True)
            graph(B - 1, False)
            sp.wait_ge(out_stored, DMA * (B * NT + 1))

        @block.tensor
        def _(pe):
            def take_bank(b, key, i):
                pe.wait_ge(acc_drained, bank_free(b, key, i))

            def transpose_h0(b, i):
                g = h0_group(b, i)
                pe.wait_ge(tp_drained, g + 1)
                pe.wait_ge(h0_ready, tile(b, i))
                for f in range(FT):
                    last = nc.tensor.transpose(tp_banks[i % TP_BANKS][:, f * P:(f + 1) * P],
                                               h0[:, i % 3, f * P:(f + 1) * P], ident_sb[:, :])
                last.then_inc(tp_full, 1)

            def product_H(ps, lhs, hi, lo, k, done=False):
                nc.tensor.matmul(ps, lhs, hi, start=(k == 0), stop=False)
                last = nc.tensor.matmul(ps, lhs, lo, start=False, stop=(k == NT - 1))
                if k == NT - 1:
                    last.then_inc(acc_full, 1)

            def c1_step(b, e, k):
                ps = acc("C1", e)
                lhs = H[:, k, e * P:(e + 1) * P]
                nc.tensor.matmul(ps[:, 0:FP], lhs, v_hi[:, k, :], start=(k == 0), stop=False)
                last = nc.tensor.matmul(ps[:, 0:F], lhs, v_lo[:, k, :], start=False, stop=(k == NT - 1))
                if k == NT - 1:
                    last.then_inc(acc_full, 1)

            def c3_step(e, k):
                product_H(acc("C3", e)[:, 0:F], H[:, k, e * P:(e + 1) * P], v_hi[:, k, 0:F], v_lo[:, k, :], k)

            def c4_step(i, k):
                product_H(acc("C4", i)[:, 0:F], HT[:, k, i * P:(i + 1) * P], g_hi[:, k, :], g_lo[:, k, :], k)

            def graph(b, more):
                for i in range(NT):
                    take_bank(b, "Z", i)
                    pe.wait_ge(tp_drained, h0_group(b, i) + 1 + TP_BANKS)
                    for f in range(FT):
                        last = nc.tensor.matmul(acc("Z", i)[:, :], h0T[:, i, f, :], w0_sb[:, f, :],
                                                start=(f == 0), stop=(f == FT - 1))
                    last.then_inc(acc_full, 1)
                for i in range(NT):
                    take_bank(b, "A", i)
                    pe.wait_ge(adjT_loaded[i % SLOTS], loaded(b, i))
                    for k in range(NT):
                        if i == 0:
                            pe.wait_ge(acc_drained, drained(b, "Z", k))
                        last = nc.tensor.matmul(acc("A", i)[:, 0:F + 1], adjT_in[:, i % SLOTS, k, :], zb[:, k, :],
                                                start=(k == 0), stop=(k == NT - 1))
                    last.then_inc(acc_full, 1)
                pe.wait_ge(H_set, tile(b, NT - 1))
                first = 4
                for e in range(first):
                    take_bank(b, "C1", e)
                    for k in range(NT - 1):
                        if e == 0:
                            pe.wait_ge(h_split, tile(b, k))
                        c1_step(b, e, k)
                pe.wait_ge(h_split, tile(b, NT - 1))
                for e in range(first):
                    c1_step(b, e, NT - 1)
                for e in range(first, NT):
                    take_bank(b, "C1", e)
                    for k in range(NT):
                        c1_step(b, e, k)
                pe.wait_ge(adjT_used, tile(b, NT - 1))
                for c in range(CH):
                    for f in range(FT):
                        n = c * FT + f
                        take_bank(b, "C2", n)
                        for k in range(NT):
                            if n == 0:
                                pe.wait_ge(acc_drained, drained(b, "C1", k))
                            rhs = HT[:, k, c * 512:(c + 1) * 512]
                            nc.tensor.matmul(acc("C2", n)[:, :], g_hi[:, k, f * P:(f + 1) * P], rhs,
                                             start=(k == 0), stop=False)
                            last = nc.tensor.matmul(acc("C2", n)[:, :], g_lo[:, k, f * P:(f + 1) * P], rhs,
                                                    start=False, stop=(k == NT - 1))
                        last.then_inc(acc_full, 1)
                for i in range(NT + 3):
                    if i < NT:
                        take_bank(b, "W1", i)
                        pe.wait_ge(acc_drained, drained(b, "C2", (i * P // 512) * FT + FT - 1))
                        for f in range(FT):
                            last = nc.tensor.matmul(acc("W1", i)[:, :], uT[:, f, i * P:(i + 1) * P], w1_sb[:, f, :],
                                                    start=(f == 0), stop=(f == FT - 1))
                        last.then_inc(acc_full, 1)
                    if 2 <= i < NT + 2:
                        j = i - 2
                        pe.wait_ge(tp_drained, hn_group(b, j) + 1)
                        pe.wait_ge(n_ready, tile(b, j))
                        for d in range(DT):
                            last = nc.tensor.transpose(tp_banks[j % TP_BANKS][:, d * P:(d + 1) * P],
                                                       t_sb[:, j % 3, d * P:(d + 1) * P], ident_sb[:, :])
                        last.then_inc(tp_full, 1)
                    if i >= 3:
                        j = i - 3
                        take_bank(b, "W2", j)
                        pe.wait_ge(tp_drained, hn_group(b, j) + 1 + TP_BANKS)
                        for d in range(DT):
                            last = nc.tensor.matmul(acc("W2", j)[:, 0:F], hnT[:, j % 2, d, :], w2_sb[:, d, :],
                                                    start=(d == 0), stop=(d == DT - 1))
                        last.then_inc(acc_full, 1)
                for e in (0, 1):
                    take_bank(b, "C3", e)
                    for k in range(NT - 1):
                        if e == 0:
                            pe.wait_ge(acc_drained, drained(b, "W2", k))
                        c3_step(e, k)
                pe.wait_ge(acc_drained, drained(b, "W2", NT - 1))
                for e in (0, 1):
                    c3_step(e, NT - 1)
                for e in range(2, NT):
                    take_bank(b, "C3", e)
                    for k in range(NT):
                        c3_step(e, k)
                    if more:
                        transpose_h0(b + 1, e - 2)
                for i in (0, 1):
                    take_bank(b, "C4", i)
                    for k in range(NT - 1):
                        if i == 0:
                            pe.wait_ge(acc_drained, drained(b, "C3", k))
                        c4_step(i, k)
                pe.wait_ge(acc_drained, drained(b, "C3", NT - 1))
                for i in (0, 1):
                    c4_step(i, NT - 1)
                for i in range(2, NT):
                    take_bank(b, "C4", i)
                    for k in range(NT):
                        c4_step(i, k)
                    if more and i < 4:
                        transpose_h0(b + 1, NT - 4 + i)

            pe.wait_ge(ident_loaded, DMA)
            for i in range(NT):
                transpose_h0(0, i)
            pe.wait_ge(w0_loaded, DMA)
            pe.wait_ge(ones_set, 3)
            pe.wait_ge(rest_loaded, 6 * DMA)
            with pe.Fori(0, B - 1) as b:
                graph(b, True)
            graph(B - 1, False)

        @block.scalar
        def _(act):
            def make_h0(b, i):
                act.wait_ge(x_ln, tile(b, i))
                if i >= 3:
                    act.wait_ge(tp_full, h0_group(b, i - 3) + 1)
                nc.scalar.activation(h0[:, i % 3, :], x_sb[:, i, :], ACT.Relu, bias=nmr[:, 0, i:i + 1],
                                     scale=rstd[:, 0, i:i + 1]).then_inc(h0_ready, 1)

            def take_h0T(b, i):
                act.wait_ge(tp_full, h0_group(b, i) + 1)
                nc.scalar.activation(h0T[:, i, :, :], tp_banks[i % TP_BANKS][:, 0:F], ACT.Copy).then_inc(tp_drained, 1)

            def graph(b, more):
                for i in range(NT):
                    act.wait_ge(acc_full, full(b, "Z", i))
                    nc.scalar.activation(za[:, i, :], acc("Z", i)[:, 0:F], ACT.Copy).then_inc(za_ready, 1)
                for i in range(NT):
                    act.wait_ge(x1_ln, tile(b, i))
                    if i >= 2:
                        act.wait_ge(h_split, tile(b, i - 2))
                        act.wait_ge(s_ready, tile(b, i - 2))
                    nc.scalar.activation(h_sb[:, i % 2, :], s_sb[:, i, :], ACT.Relu, bias=nmr[:, 1, i:i + 1],
                                         scale=rstd[:, 1, i:i + 1])
                    nc.scalar.activation(v_hi[:, i, 0:F], s_sb[:, i, :], ACT.Relu, bias=nmr[:, 1, i:i + 1],
                                         scale=rstd[:, 1, i:i + 1]).then_inc(h_ready, 1)
                for e in range(NT):
                    act.wait_ge(b_ready, tile(b, e))
                    nc.scalar.activation(g_hi[:, e, :], acc("C1", e)[:, 0:F], ACT.Copy,
                                         scale=b_inv[:, e:e + 1]).then_inc(g_hi_ready, 1)
                for i in range(2, NT + 3):
                    if i < NT + 2:
                        j = i - 2
                        act.wait_ge(tp_full, hn_group(b, j) + 1)
                        for d in range(DT):
                            last = nc.scalar.activation(hnT[:, j % 2, d, :], tp_banks[j % TP_BANKS][:, d * P:(d + 1) * P],
                                                        ACT.Identity, bias=beta_sb[:, d:d + 1],
                                                        scale=gamma_sb[:, d:d + 1])
                        last.then_inc(tp_drained, 1)
                    if i >= 3:
                        j = i - 3
                        act.wait_ge(acc_full, full(b, "W2", j))
                        nc.scalar.activation(v_hi[:, j, 0:F], acc("W2", j)[:, 0:F], ACT.Copy).then_inc(y_hi_ready, 1)
                for e in range(NT):
                    act.wait_ge(acc_full, full(b, "C3", e))
                    nc.scalar.activation(g_hi[:, e, :], acc("C3", e)[:, 0:F], ACT.Copy,
                                         scale=b_inv[:, e:e + 1]).then_inc(g_hi_ready, 1)
                    if more:
                        if e >= 3:
                            take_h0T(b + 1, e - 3)
                        make_h0(b + 1, e)
                if more:
                    for i in range(NT - 3, NT):
                        take_h0T(b + 1, i)

            act.sem_inc(tp_drained, TP_BANKS)
            for i in range(NT):
                make_h0(0, i)
                if i >= 1:
                    take_h0T(0, i - 1)
            take_h0T(0, NT - 1)
            act.wait_ge(rest_loaded, 6 * DMA)
            with act.Fori(0, B - 1) as b:
                graph(b, True)
            graph(B - 1, False)

        @block.gpsimd
        def _(pool):
            def inverse_std(b, i, ln, mv, moments, ve_sem, rstd_sem):
                pool.wait_ge(moments, tile(b, i))
                if ln < 2:
                    nc.gpsimd.tensor_tensor(neg_mean[:, ln, i:i + 1], zero[:, :], mv[:, i, 0:1], ALU.subtract)
                nc.gpsimd.tensor_tensor(ve[:, ln, i:i + 1], mv[:, i, 1:2], eps[:, :], ALU.add).then_inc(ve_sem, 1)
                pool.wait_ge(ve_sem, tile(b, i))
                nc.gpsimd.tensor_tensor(rstd[:, ln, i:i + 1], ve[:, ln, i:i + 1], neg_half[:, :],
                                        ALU.pow).then_inc(rstd_sem, 1)

            def shift(b, i, ln, rstd_sem, ln_sem):
                pool.wait_ge(rstd_sem, tile(b, i))
                nc.gpsimd.tensor_tensor(nmr[:, ln, i:i + 1], neg_mean[:, ln, i:i + 1], rstd[:, ln, i:i + 1],
                                        ALU.mult).then_inc(ln_sem, 1)

            def ln_x(b, i):
                inverse_std(b, i, 0, x_mv, x_moments, x_ve, x_rstd)
                shift(b, i, 0, x_rstd, x_ln)

            def residual(b, i):
                pool.wait_ge(h_ready, tile(b, i))
                nc.gpsimd.tensor_tensor(s_sb[:, i, :], s_sb[:, i, :], b2_sb[:, :], ALU.add).then_inc(s_biased, 1)
                pool.wait_ge(s_biased, tile(b, i))
                nc.gpsimd.tensor_tensor(s_sb[:, i, :], s_sb[:, i, :], h_sb[:, i % 2, :], ALU.add).then_inc(s_ready, 1)

            def graph(b, more):
                for i in range(NT):
                    inverse_std(b, i, 1, x1_mv, x1_moments, x1_ve, x1_rstd)
                    shift(b, i, 1, x1_rstd, x1_ln)
                    if i >= 1:
                        residual(b, i - 1)
                residual(b, NT - 1)
                for i in range(NT):
                    inverse_std(b, i, 2, t_mv, t_moments, t_ve, t_rstd)
                    if more:
                        ln_x(b + 1, i)

            nc.gpsimd.memset(zero[:, :], 0.0).then_inc(consts_set, 1)
            nc.gpsimd.memset(eps[:, :], LN_EPS).then_inc(consts_set, 1)
            nc.gpsimd.memset(neg_half[:, :], -0.5).then_inc(consts_set, 1)
            pool.wait_ge(consts_set, 3)
            for i in range(NT):
                ln_x(0, i)
            pool.wait_ge(rest_loaded, 6 * DMA)
            with pool.Fori(0, B - 1) as b:
                graph(b, True)
            graph(B - 1, False)

        @block.vector
        def _(dve):
            def stats_x(b, i):
                dve.wait_ge(x_loaded, b * DMA + DMA)
                nc.vector.bn_stats(x_st[:, i, :], x_sb[:, i, :]).then_inc(x_stats, 1)

            def moments_x(i):
                nc.vector.bn_aggr(x_mv[:, i, :], x_st[:, i, :]).then_inc(x_moments, 1)

            def mask_rows(b, i):
                dve.wait_ge(adj_loaded[i % SLOTS], loaded(b, i))
                if i == 0:
                    dve.wait_ge(wrow_loaded, b * DMA + DMA)
                slot = adj_in[:, i % SLOTS, :]
                nc.vector.tensor_scalar(H[:, i, :], slot, 0.0, None, ALU.not_equal).then_inc(H_set, 1)
                dve.wait_ge(H_set, tile(b, i))
                nc.vector.scalar_tensor_tensor(out=slot, in0=slot, scalar=0.0, in1=wrow[:, :], op0=ALU.not_equal,
                                               op1=ALU.mult, accum_out=d_sum[:, i:i + 1]).then_inc(adj_used, 1)

            def invert_d(b):
                dve.wait_ge(adj_used, tile(b, NT - 1))
                nc.vector.tensor_scalar(d_pos[:, :], d_sum[:, :], 0.0, None, ALU.is_gt).then_inc(d_positive, 1)
                nc.vector.tensor_scalar(d_safe[:, :], d_sum[:, :], TINY, None, ALU.max).then_inc(d_guarded, 1)
                dve.wait_ge(d_guarded, b + 1)
                nc.vector.reciprocal(d_rec[:, :], d_safe[:, :]).then_inc(d_divided, 1)
                dve.wait_ge(d_divided, b + 1)
                nc.vector.tensor_tensor(d_inv[:, :], d_rec[:, :], d_pos[:, :], ALU.mult).then_inc(d_ready, 1)

            def split_h(b, i):
                dve.wait_ge(h_ready, tile(b, i))
                nc.vector.tensor_tensor(v_lo[:, i, :], h_sb[:, i % 2, :], v_hi[:, i, 0:F].bitcast(F32),
                                        ALU.subtract).then_inc(h_split, 1)

            def split_g(key, e, parts):
                dve.wait_ge(g_hi_ready, parts)
                nc.vector.scalar_tensor_tensor(out=g_lo[:, e, :], in0=acc(key, e)[:, 0:F], scalar=b_inv[:, e:e + 1],
                                               in1=g_hi[:, e, :].bitcast(F32), op0=ALU.mult,
                                               op1=ALU.subtract).then_inc(acc_drained, 1)

            def graph(b, more):
                for i in range(NT):
                    dve.wait_ge(acc_full, full(b, "Z", i))
                    dve.wait_ge(za_ready, tile(b, i))
                    nc.vector.tensor_copy(zb[:, i, 0:F], acc("Z", i)[:, F:2 * F]).then_inc(acc_drained, 1)
                    if i % 2 == 0:
                        mask_rows(b, NT // 2 + i // 2)
                invert_d(b)
                for i in range(NT):
                    ps = acc("A", i)
                    dve.wait_ge(acc_full, full(b, "A", i))
                    nc.vector.tensor_scalar(deg[:, i:i + 1], ps[:, F:F + 1], DEG_EPS, None,
                                            ALU.max).then_inc(deg_guarded, 1)
                    dve.wait_ge(deg_guarded, tile(b, i))
                    nc.vector.reciprocal(deg_inv[:, i:i + 1], deg[:, i:i + 1]).then_inc(deg_divided, 1)
                    dve.wait_ge(deg_divided, tile(b, i))
                    nc.vector.scalar_tensor_tensor(out=u_sb[:, i % 2, :], in0=ps[:, 0:F], scalar=deg_inv[:, i:i + 1],
                                                   in1=za[:, i, :], op0=ALU.mult, op1=ALU.add).then_inc(acc_drained, 1)
                    dve.wait_ge(acc_drained, drained(b, "A", i))
                    if i == 0:
                        dve.wait_ge(out_stored, b * (DMA * NT) + DMA)
                    nc.vector.scalar_tensor_tensor(out=s_sb[:, i, :], in0=u_sb[:, i % 2, :], scalar=0.0,
                                                   in1=x_sb[:, i, :], op0=ALU.max, op1=ALU.add).then_inc(x1_ready, 1)
                    dve.wait_ge(x1_ready, tile(b, i))
                    nc.vector.bn_stats(x1_st[:, i, :], s_sb[:, i, :]).then_inc(x1_stats, 1)
                    dve.wait_ge(ones_set, 3)
                    dve.wait_ge(x1_stats, tile(b, i))
                    nc.vector.bn_aggr(x1_mv[:, i, :], x1_st[:, i, :]).then_inc(x1_moments, 1)
                    dve.wait_ge(adjT_loaded[i % SLOTS], loaded(b, i))
                    nc.vector.tensor_scalar(HT[:, :, i * P:(i + 1) * P], adjT_in[:, i % SLOTS, :, :], 0.0, None,
                                            ALU.not_equal).then_inc(adjT_used, 1)
                    if i >= 1:
                        split_h(b, i - 1)
                split_h(b, NT - 1)
                for e in range(NT):
                    dve.wait_ge(acc_full, full(b, "C1", e))
                    nc.vector.tensor_scalar(cnt[:, e:e + 1], acc("C1", e)[:, F:F + 1], 1.0, None,
                                            ALU.max).then_inc(cnt_guarded, 1)
                    dve.wait_ge(cnt_guarded, tile(b, e))
                    nc.vector.reciprocal(b_inv[:, e:e + 1], cnt[:, e:e + 1]).then_inc(b_ready, 1)
                    dve.wait_ge(b_ready, tile(b, e))
                    split_g("C1", e, b * (2 * NT) + (e + 1))
                for c in range(CH):
                    for f in range(FT):
                        n = c * FT + f
                        dve.wait_ge(acc_full, full(b, "C2", n))
                        nc.vector.tensor_copy(uT[:, f, c * 512:(c + 1) * 512], acc("C2", n)[:, :]).then_inc(acc_drained, 1)
                dve.wait_ge(d_ready, b + 1)
                for i in range(NT + 3):
                    if i < NT:
                        dve.wait_ge(acc_full, full(b, "W1", i))
                        nc.vector.scalar_tensor_tensor(out=v1_sb[:, :], in0=acc("W1", i)[:, :], scalar=d_inv[:, i:i + 1],
                                                       in1=b1_sb[:, :], op0=ALU.mult,
                                                       op1=ALU.add).then_inc(acc_drained, 1)
                        if more:
                            stats_x(b + 1, i)
                            dve.wait_ge(x_stats, tile(b + 1, i))
                        dve.wait_ge(acc_drained, drained(b, "W1", i))
                        if i >= 3:
                            dve.wait_ge(tp_full, hn_group(b, i - 3) + 1)
                        nc.vector.tensor_scalar(t_sb[:, i % 3, :], v1_sb[:, :], 0.0, None, ALU.max).then_inc(t_ready, 1)
                        if more:
                            moments_x(i)
                        dve.wait_ge(t_ready, tile(b, i))
                        nc.vector.bn_stats(t_st[:, i, :], t_sb[:, i % 3, :]).then_inc(t_stats, 1)
                        dve.wait_ge(ones_set, 3)
                        dve.wait_ge(t_stats, tile(b, i))
                        nc.vector.bn_aggr(t_mv[:, i, :], t_st[:, i, :]).then_inc(t_moments, 1)
                    if 1 <= i <= NT:
                        j = i - 1
                        dve.wait_ge(t_rstd, tile(b, j))
                        nc.vector.tensor_scalar(t_sb[:, j % 3, :], t_sb[:, j % 3, :], t_mv[:, j, 0:1],
                                                rstd[:, 2, j:j + 1], ALU.subtract, ALU.mult).then_inc(n_ready, 1)
                    if i >= 3:
                        j = i - 3
                        dve.wait_ge(y_hi_ready, tile(b, j))
                        nc.vector.tensor_tensor(v_lo[:, j, :], acc("W2", j)[:, 0:F], v_hi[:, j, 0:F].bitcast(F32),
                                                ALU.subtract).then_inc(acc_drained, 1)
                for e in range(NT):
                    split_g("C3", e, b * (2 * NT) + (NT + e + 1))
                for i in range(NT):
                    dve.wait_ge(acc_full, full(b, "C4", i))
                    dve.wait_ge(s_ready, tile(b, i))
                    nc.vector.scalar_tensor_tensor(out=s_sb[:, i, :], in0=acc("C4", i)[:, 0:F], scalar=d_inv[:, i:i + 1],
                                                   in1=s_sb[:, i, :], op0=ALU.mult, op1=ALU.add).then_inc(acc_drained, 1)
                    if more and i % 2 == 0:
                        mask_rows(b + 1, i // 2)

            nc.vector.memset(zb[:, :, F:F + 1], 1.0).then_inc(ones_set, 1)
            nc.vector.memset(v_hi[:, :, F:F + 1].bitcast(F32), 1.0).then_inc(ones_set, 1)
            nc.vector.memset(v_hi[:, :, F + 1:F + 2].bitcast(F32), 0.0).then_inc(ones_set, 1)
            dve.sem_inc(acc_drained, ACC_BANKS)
            for i in range(NT):
                stats_x(0, i)
                dve.wait_ge(x_stats, tile(0, i))
                moments_x(i)
            for i in range(NT // 2):
                mask_rows(0, i)
            dve.wait_ge(rest_loaded, 6 * DMA)
            with dve.Fori(0, B - 1) as b:
                graph(b, True)
            graph(B - 1, False)


def kernel(x, adj, L0_gnn_W, L1_gnn_W1, L1_gnn_b1, L1_gnn_gamma, L1_gnn_beta, L1_gnn_W2, L1_gnn_b2):
    import numpy as np
    import concourse.bacc as bacc
    from concourse.bass_utils import run_bass_kernel_spmd

    x, adj = np.ascontiguousarray(x), np.ascontiguousarray(adj)
    B, N, _ = adj.shape
    F = x.shape[2]
    NT = N // P

    def rows_on_partitions(a):
        a = np.asarray(a)
        return np.ascontiguousarray(a.reshape(-1, P, a.shape[1]).transpose(1, 0, 2))

    def spread(v):
        return np.ascontiguousarray(np.broadcast_to(np.asarray(v), (P, len(v))))

    def per_partition(v):
        return np.ascontiguousarray(np.asarray(v).reshape(-1, P).T)

    W = np.asarray(L0_gnn_W)
    arrays = {
        "x": x,
        "adj": adj,
        "adj_t": np.ascontiguousarray(adj.reshape(B, NT, P, NT, P).transpose(0, 1, 4, 3, 2)),
        "w0": rows_on_partitions(np.concatenate([W[:, :F].T, W[:, F:].T], axis=1)),
        "w1": rows_on_partitions(np.asarray(L1_gnn_W1).T),
        "w2": rows_on_partitions(np.asarray(L1_gnn_W2).T),
        "b1": spread(L1_gnn_b1),
        "b2": spread(L1_gnn_b2),
        "gamma": per_partition(L1_gnn_gamma),
        "beta": per_partition(L1_gnn_beta),
        "ident": np.eye(P, dtype=np.float32),
    }
    nc = bacc.Bacc("TRN2", target_bir_lowering=False, num_devices=1)
    args = [nc.dram_tensor(f"in_{k}", a.shape, mybir.dt.from_np(a.dtype), kind="ExternalInput").ap()
            for k, a in arrays.items()]
    out = nc.dram_tensor("out", x.shape, F32, kind="ExternalOutput").ap()
    build(nc, *args, out)
    r = run_bass_kernel_spmd(nc, [{f"in_{k}": a for k, a in arrays.items()}], core_ids=[0])
    return r.results[0]["out"]
```

```python
from contextlib import ExitStack

import concourse.bass as bass
from concourse import mybir
from concourse.alu_op_type import AluOpType as ALU


F32 = mybir.dt.float32
F32R = mybir.dt.float32r
ACT = mybir.ActivationFunctionType

P = 128
ACC_BANKS = 6
TP_BANKS = 2
SLOTS = 4
X_PARTS = 4
T_LAG = 3
EARLY = 4
DEG_EPS = 1e-6
LN_EPS = 1e-5
TINY = 1.1754944e-38
DMA = 16


def acc_order(NT, chunks, FT):
    order = [("Z", i) for i in range(NT)] + [("A", i) for i in range(NT)] + [("C1", i) for i in range(NT)]
    order += [("C2", c * FT + f) for c in range(chunks) for f in range(FT)]
    for i in range(NT + T_LAG + 1):
        if i < NT:
            order.append(("W1", i))
        if i > T_LAG:
            order.append(("W2", i - T_LAG - 1))
    order += [("C3", i) for i in range(NT)] + [("C4", i) for i in range(NT)]
    return {key: n for n, key in enumerate(order)}


def build(nc, x, adj, adj_t, w0, w1, w2, b1, b2, gamma, beta, ident, out):
    B, N, _ = adj.shape
    F = x.shape[2]
    D = w1.shape[2]
    NT = N // P
    FT = F // P
    DT = D // P
    CH = N // 512
    FP = F + 2
    NUM = acc_order(NT, CH, FT)
    PER = len(NUM)
    TPS = 2 * NT
    assert PER % ACC_BANKS == 0 and TPS % TP_BANKS == 0 and NT % SLOTS == 0 and D == 512

    with ExitStack() as ctx:
        def sb(name, shape, dt=F32):
            return ctx.enter_context(nc.sbuf_tensor(name, shape, dt))

        def sem(name):
            return ctx.enter_context(nc.semaphore(name))

        adj_in = sb("adj_in", [P, SLOTS, N])
        adjT_in = sb("adjT_in", [P, SLOTS, NT, P])
        H = sb("H", [P, NT, N], F32R)
        HT = sb("HT", [P, NT, N], F32R)
        x_sb = sb("x_sb", [P, NT, F])
        s_sb = sb("s_sb", [P, NT, F])
        fbuf = sb("fbuf", [P, NT * F])
        zb = sb("zb", [P, NT, F + 1])
        v_hi = sb("v_hi", [P, NT, FP], F32R)
        v_lo = sb("v_lo", [P, NT, F], F32R)
        g_hi = sb("g_hi", [P, NT, F], F32R)
        g_lo = sb("g_lo", [P, NT, F], F32R)
        w0_sb = sb("w0_sb", [P, FT, 2 * F])
        w1_sb = sb("w1_sb", [P, FT, D])
        w2_sb = sb("w2_sb", [P, DT, F])
        b1_sb = sb("b1_sb", [P, D])
        b2_sb = sb("b2_sb", [P, F])
        gamma_sb = sb("gamma_sb", [P, DT])
        beta_sb = sb("beta_sb", [P, DT])
        ident_sb = sb("ident_sb", [P, P])
        wrow = sb("wrow", [P, N])
        h0 = sb("h0", [P, 3, F])
        u_sb = sb("u_sb", [P, 2, F])
        h_sb = sb("h_sb", [P, 2, F])
        v1_sb = sb("v1_sb", [P, D])
        t_sb = sb("t_sb", [P, T_LAG + 1, D])
        hnT = sb("hnT", [P, 2, DT, P])
        neg_half = sb("neg_half", [P, 1])
        zero = sb("zero", [P, 1])
        eps = sb("eps", [P, 1])
        neg_mean = sb("neg_mean", [P, 2, NT])
        x_st = sb("x_st", [P, NT, 6])
        x_mv = sb("x_mv", [P, NT, 2])
        x1_st = sb("x1_st", [P, NT, 6])
        x1_mv = sb("x1_mv", [P, NT, 2])
        t_st = sb("t_st", [P, NT, 6])
        t_mv = sb("t_mv", [P, NT, 2])
        ve = sb("ve", [P, 3, NT])
        rstd = sb("rstd", [P, 3, NT])
        nmr = sb("nmr", [P, 2, NT])
        deg = sb("deg", [P, NT])
        deg_inv = sb("deg_inv", [P, NT])
        cnt = sb("cnt", [P, NT])
        b_inv = sb("b_inv", [P, NT])
        d_sum = sb("d_sum", [P, NT])
        d_pos = sb("d_pos", [P, NT])
        d_safe = sb("d_safe", [P, NT])
        d_rec = sb("d_rec", [P, NT])
        d_inv = sb("d_inv", [P, NT])

        h0T = fbuf[:, :].rearrange("p (i f n) -> p i f n", i=NT, f=FT)
        za = fbuf[:, :].rearrange("p (i f) -> p i f", i=NT)
        uT = fbuf[:, :].rearrange("p (f n) -> p f n", f=FT)

        acc_banks = [ctx.enter_context(nc.psum_tensor(f"acc{k}", [P, 512], F32)) for k in range(ACC_BANKS)]
        tp_banks = [ctx.enter_context(nc.psum_tensor(f"tp{k}", [P, 512], F32)) for k in range(TP_BANKS)]

        def acc(key, i):
            return acc_banks[NUM[key, i] % ACC_BANKS]

        adj_loaded = [sem(f"adj_loaded{k}") for k in range(SLOTS)]
        adjT_loaded = [sem(f"adjT_loaded{k}") for k in range(SLOTS)]
        x_loaded = [sem(f"x_loaded{k}") for k in range(X_PARTS)]
        wrow_loaded = sem("wrow_loaded")
        ident_loaded = sem("ident_loaded")
        w0_loaded = sem("w0_loaded")
        w12_loaded = sem("w12_loaded")
        rows_loaded = sem("rows_loaded")
        out_stored = sem("out_stored")
        acc_full = sem("acc_full")
        acc_drained = sem("acc_drained")
        tp_full = sem("tp_full")
        tp_drained = sem("tp_drained")
        ones_set = sem("ones_set")
        consts_set = sem("consts_set")
        x_stats = sem("x_stats")
        x_moments = sem("x_moments")
        x_ve = sem("x_ve")
        x_rstd = sem("x_rstd")
        x_ln = sem("x_ln")
        h0_ready = sem("h0_ready")
        H_set = sem("H_set")
        adj_used = sem("adj_used")
        d_positive = sem("d_positive")
        d_guarded = sem("d_guarded")
        d_divided = sem("d_divided")
        d_ready = sem("d_ready")
        za_ready = sem("za_ready")
        deg_guarded = sem("deg_guarded")
        deg_divided = sem("deg_divided")
        x1_ready = sem("x1_ready")
        x1_stats = sem("x1_stats")
        x1_moments = sem("x1_moments")
        x1_ve = sem("x1_ve")
        x1_rstd = sem("x1_rstd")
        x1_ln = sem("x1_ln")
        h_ready = sem("h_ready")
        h_split = sem("h_split")
        s_biased = sem("s_biased")
        s_ready = sem("s_ready")
        adjT_used = sem("adjT_used")
        cnt_guarded = sem("cnt_guarded")
        b_ready = sem("b_ready")
        g_hi_ready = sem("g_hi_ready")
        t_ready = sem("t_ready")
        t_stats = sem("t_stats")
        t_moments = sem("t_moments")
        t_ve = sem("t_ve")
        t_rstd = sem("t_rstd")
        n_ready = sem("n_ready")
        y_hi_ready = sem("y_hi_ready")

        def tile(b, i):
            return b * NT + (i + 1)

        def full(b, key, i):
            return b * PER + (NUM[key, i] + 1)

        def drained(b, key, i):
            return b * PER + (NUM[key, i] + 1 + ACC_BANKS)

        def bank_free(b, key, i):
            return b * PER + (NUM[key, i] + 1)

        def hn_group(b, i):
            return b * TPS + (NT + i)

        def h0_group(b, i):
            return b * TPS + i

        def loaded(b, i):
            return b * (DMA * NT // SLOTS) + DMA * (i // SLOTS + 1)

        block = ctx.enter_context(nc.Block())

        @block.sync
        def _(sp):
            def load_adj(b, i):
                sp.dma_start(adj_in[:, i % SLOTS, :], adj[b, i * P:(i + 1) * P, :]).then_inc(adj_loaded[i % SLOTS], DMA)

            def load_adjT(b, i):
                sp.dma_start(adjT_in[:, i % SLOTS, :, :], adj_t[b, i]).then_inc(adjT_loaded[i % SLOTS], DMA)

            def load_x(b):
                w = NT // X_PARTS
                for k in range(X_PARTS):
                    part = x[b, k * w * P:(k + 1) * w * P, :].rearrange("(i p) f -> p i f", p=P)
                    sp.dma_start(x_sb[:, k * w:(k + 1) * w, :], part).then_inc(x_loaded[k], DMA)

            def load_wrow(b):
                sp.dma_start(wrow[:, :], adj[b, 0:1, :].to_broadcast([P, N])).then_inc(wrow_loaded, DMA)

            sp.sem_inc(out_stored, DMA)
            load_x(0)
            sp.dma_start(ident_sb[:, :], ident).then_inc(ident_loaded, DMA)
            sp.dma_start(w0_sb[:, :, :], w0).then_inc(w0_loaded, DMA)
            load_wrow(0)
            for i in range(SLOTS):
                load_adj(0, i)
            for i in range(SLOTS):
                load_adjT(0, i)
            for dst, src in ((b1_sb, b1), (b2_sb, b2), (gamma_sb, gamma), (beta_sb, beta)):
                sp.dma_start(dst[:, :], src).then_inc(rows_loaded, DMA)
            for dst, src in ((w1_sb, w1), (w2_sb, w2)):
                sp.dma_start(dst[:, :, :], src).then_inc(w12_loaded, DMA)

            def graph(b, more):
                for i in range(SLOTS, NT):
                    sp.wait_ge(adj_used, tile(b, i - SLOTS))
                    load_adj(b, i)
                for i in range(SLOTS, NT):
                    sp.wait_ge(adjT_used, tile(b, i - SLOTS))
                    load_adjT(b, i)
                if more:
                    for i in range(SLOTS):
                        sp.wait_ge(adj_used, tile(b, NT - SLOTS + i))
                        load_adj(b + 1, i)
                    load_wrow(b + 1)
                    for i in range(SLOTS):
                        sp.wait_ge(adjT_used, tile(b, NT - SLOTS + i))
                        load_adjT(b + 1, i)
                    sp.wait_ge(x1_ready, tile(b, NT - 1))
                    load_x(b + 1)
                for i in range(NT):
                    sp.wait_ge(acc_drained, drained(b, "C4", i))
                    sp.dma_start(out[b, i * P:(i + 1) * P, :], s_sb[:, i, :]).then_inc(out_stored, DMA)

            with sp.Fori(0, B - 1) as b:
                graph(b, True)
            graph(B - 1, False)
            sp.wait_ge(out_stored, DMA * (B * NT + 1))

        @block.tensor
        def _(pe):
            def take_bank(b, key, i):
                pe.wait_ge(acc_drained, bank_free(b, key, i))

            def transpose_h0(b, i):
                g = h0_group(b, i)
                pe.wait_ge(tp_drained, g + 1)
                pe.wait_ge(h0_ready, tile(b, i))
                for f in range(FT):
                    last = nc.tensor.transpose(tp_banks[i % TP_BANKS][:, f * P:(f + 1) * P],
                                               h0[:, i % 3, f * P:(f + 1) * P], ident_sb[:, :])
                last.then_inc(tp_full, 1)

            def product_H(ps, lhs, hi, lo, k, done=False):
                nc.tensor.matmul(ps, lhs, hi, start=(k == 0), stop=False)
                last = nc.tensor.matmul(ps, lhs, lo, start=False, stop=(k == NT - 1))
                if k == NT - 1:
                    last.then_inc(acc_full, 1)

            def c1_step(b, e, k):
                ps = acc("C1", e)
                lhs = H[:, k, e * P:(e + 1) * P]
                nc.tensor.matmul(ps[:, 0:FP], lhs, v_hi[:, k, :], start=(k == 0), stop=False)
                last = nc.tensor.matmul(ps[:, 0:F], lhs, v_lo[:, k, :], start=False, stop=(k == NT - 1))
                if k == NT - 1:
                    last.then_inc(acc_full, 1)

            def c3_step(e, k):
                product_H(acc("C3", e)[:, 0:F], H[:, k, e * P:(e + 1) * P], v_hi[:, k, 0:F], v_lo[:, k, :], k)

            def c4_step(i, k):
                product_H(acc("C4", i)[:, 0:F], HT[:, k, i * P:(i + 1) * P], g_hi[:, k, :], g_lo[:, k, :], k)

            def graph(b, more):
                for i in range(NT):
                    take_bank(b, "Z", i)
                    pe.wait_ge(tp_drained, h0_group(b, i) + 1 + TP_BANKS)
                    for f in range(FT):
                        last = nc.tensor.matmul(acc("Z", i)[:, :], h0T[:, i, f, :], w0_sb[:, f, :],
                                                start=(f == 0), stop=(f == FT - 1))
                    last.then_inc(acc_full, 1)
                    if i < NT - EARLY:
                        transpose_h0(b, EARLY + i)
                for i in range(NT):
                    take_bank(b, "A", i)
                    pe.wait_ge(adjT_loaded[i % SLOTS], loaded(b, i))
                    for k in range(NT):
                        if i == 0:
                            pe.wait_ge(acc_drained, drained(b, "Z", k))
                        last = nc.tensor.matmul(acc("A", i)[:, 0:F + 1], adjT_in[:, i % SLOTS, k, :], zb[:, k, :],
                                                start=(k == 0), stop=(k == NT - 1))
                    last.then_inc(acc_full, 1)
                pe.wait_ge(H_set, tile(b, NT - 1))
                first = ACC_BANKS
                for e in range(first):
                    take_bank(b, "C1", e)
                    for k in range(NT - 2):
                        if e == 0:
                            pe.wait_ge(h_split, tile(b, k))
                        c1_step(b, e, k)
                for k in (NT - 2, NT - 1):
                    pe.wait_ge(h_split, tile(b, k))
                    for e in range(first):
                        c1_step(b, e, k)
                for e in range(first, NT):
                    take_bank(b, "C1", e)
                    for k in range(NT):
                        c1_step(b, e, k)
                pe.wait_ge(adjT_used, tile(b, NT - 1))
                for c in range(CH):
                    for f in range(FT):
                        n = c * FT + f
                        take_bank(b, "C2", n)
                        for k in range(NT):
                            if n == 0:
                                pe.wait_ge(acc_drained, drained(b, "C1", k))
                            rhs = HT[:, k, c * 512:(c + 1) * 512]
                            nc.tensor.matmul(acc("C2", n)[:, :], g_hi[:, k, f * P:(f + 1) * P], rhs,
                                             start=(k == 0), stop=False)
                            last = nc.tensor.matmul(acc("C2", n)[:, :], g_lo[:, k, f * P:(f + 1) * P], rhs,
                                                    start=False, stop=(k == NT - 1))
                        last.then_inc(acc_full, 1)
                pe.wait_ge(w12_loaded, 2 * DMA)
                for i in range(NT + T_LAG + 1):
                    if i < NT:
                        take_bank(b, "W1", i)
                        pe.wait_ge(acc_drained, drained(b, "C2", (i * P // 512) * FT + FT - 1))
                        for f in range(FT):
                            last = nc.tensor.matmul(acc("W1", i)[:, :], uT[:, f, i * P:(i + 1) * P], w1_sb[:, f, :],
                                                    start=(f == 0), stop=(f == FT - 1))
                        last.then_inc(acc_full, 1)
                    if T_LAG <= i < NT + T_LAG:
                        j = i - T_LAG
                        pe.wait_ge(tp_drained, hn_group(b, j) + 1)
                        pe.wait_ge(n_ready, tile(b, j))
                        for d in range(DT):
                            last = nc.tensor.transpose(tp_banks[j % TP_BANKS][:, d * P:(d + 1) * P],
                                                       t_sb[:, j % (T_LAG + 1), d * P:(d + 1) * P], ident_sb[:, :])
                        last.then_inc(tp_full, 1)
                    if i > T_LAG:
                        j = i - T_LAG - 1
                        take_bank(b, "W2", j)
                        pe.wait_ge(tp_drained, hn_group(b, j) + 1 + TP_BANKS)
                        for d in range(DT):
                            last = nc.tensor.matmul(acc("W2", j)[:, 0:F], hnT[:, j % 2, d, :], w2_sb[:, d, :],
                                                    start=(d == 0), stop=(d == DT - 1))
                        last.then_inc(acc_full, 1)
                for e in (0, 1):
                    take_bank(b, "C3", e)
                    for k in range(NT - 1):
                        if e == 0:
                            pe.wait_ge(acc_drained, drained(b, "W2", k))
                        c3_step(e, k)
                pe.wait_ge(acc_drained, drained(b, "W2", NT - 1))
                for e in (0, 1):
                    c3_step(e, NT - 1)
                for e in range(2, NT):
                    take_bank(b, "C3", e)
                    for k in range(NT):
                        c3_step(e, k)
                    if more and e >= 4:
                        transpose_h0(b + 1, e - 4)
                for i in (0, 1):
                    take_bank(b, "C4", i)
                    for k in range(NT - 1):
                        if i == 0:
                            pe.wait_ge(acc_drained, drained(b, "C3", k))
                        c4_step(i, k)
                pe.wait_ge(acc_drained, drained(b, "C3", NT - 1))
                for i in (0, 1):
                    c4_step(i, NT - 1)
                for i in range(2, NT):
                    take_bank(b, "C4", i)
                    for k in range(NT):
                        c4_step(i, k)

            pe.wait_ge(ident_loaded, DMA)
            for i in range(EARLY):
                transpose_h0(0, i)
            pe.wait_ge(w0_loaded, DMA)
            pe.wait_ge(ones_set, 3)
            with pe.Fori(0, B - 1) as b:
                graph(b, True)
            graph(B - 1, False)

        @block.scalar
        def _(act):
            def make_h0(b, i):
                act.wait_ge(x_ln, tile(b, i))
                if i >= 3:
                    act.wait_ge(tp_full, h0_group(b, i - 3) + 1)
                nc.scalar.activation(h0[:, i % 3, :], x_sb[:, i, :], ACT.Relu, bias=nmr[:, 0, i:i + 1],
                                     scale=rstd[:, 0, i:i + 1]).then_inc(h0_ready, 1)

            def take_h0T(b, i):
                act.wait_ge(tp_full, h0_group(b, i) + 1)
                nc.scalar.activation(h0T[:, i, :, :], tp_banks[i % TP_BANKS][:, 0:F], ACT.Copy).then_inc(tp_drained, 1)

            def graph(b, more):
                for i in range(NT):
                    act.wait_ge(acc_full, full(b, "Z", i))
                    nc.scalar.activation(za[:, i, :], acc("Z", i)[:, 0:F], ACT.Copy).then_inc(za_ready, 1)
                    if i < NT - EARLY:
                        take_h0T(b, EARLY + i)
                        if i + 1 < NT - EARLY:
                            make_h0(b, EARLY + i + 1)
                for i in range(NT):
                    act.wait_ge(x1_ln, tile(b, i))
                    if i >= 2:
                        act.wait_ge(h_split, tile(b, i - 2))
                        act.wait_ge(s_ready, tile(b, i - 2))
                    nc.scalar.activation(h_sb[:, i % 2, :], s_sb[:, i, :], ACT.Relu, bias=nmr[:, 1, i:i + 1],
                                         scale=rstd[:, 1, i:i + 1])
                    nc.scalar.activation(v_hi[:, i, 0:F], s_sb[:, i, :], ACT.Relu, bias=nmr[:, 1, i:i + 1],
                                         scale=rstd[:, 1, i:i + 1]).then_inc(h_ready, 1)
                for e in range(NT):
                    act.wait_ge(b_ready, tile(b, e))
                    nc.scalar.activation(g_hi[:, e, :], acc("C1", e)[:, 0:F], ACT.Copy,
                                         scale=b_inv[:, e:e + 1]).then_inc(g_hi_ready, 1)
                act.wait_ge(rows_loaded, 4 * DMA)
                for i in range(T_LAG, NT + T_LAG + 1):
                    if i < NT + T_LAG:
                        j = i - T_LAG
                        act.wait_ge(tp_full, hn_group(b, j) + 1)
                        for d in range(DT):
                            last = nc.scalar.activation(hnT[:, j % 2, d, :], tp_banks[j % TP_BANKS][:, d * P:(d + 1) * P],
                                                        ACT.Identity, bias=beta_sb[:, d:d + 1],
                                                        scale=gamma_sb[:, d:d + 1])
                        last.then_inc(tp_drained, 1)
                    if i > T_LAG:
                        j = i - T_LAG - 1
                        act.wait_ge(acc_full, full(b, "W2", j))
                        nc.scalar.activation(v_hi[:, j, 0:F], acc("W2", j)[:, 0:F], ACT.Copy).then_inc(y_hi_ready, 1)
                for e in range(NT):
                    act.wait_ge(acc_full, full(b, "C3", e))
                    nc.scalar.activation(g_hi[:, e, :], acc("C3", e)[:, 0:F], ACT.Copy,
                                         scale=b_inv[:, e:e + 1]).then_inc(g_hi_ready, 1)
                    if more:
                        if 1 <= e <= EARLY + 1:
                            make_h0(b + 1, e - 1)
                        if e >= NT - EARLY:
                            take_h0T(b + 1, e - (NT - EARLY))

            act.sem_inc(tp_drained, TP_BANKS)
            for i in range(EARLY + 1):
                make_h0(0, i)
                if i >= 1:
                    take_h0T(0, i - 1)
            with act.Fori(0, B - 1) as b:
                graph(b, True)
            graph(B - 1, False)

        @block.gpsimd
        def _(pool):
            def inverse_std(b, i, ln, mv, moments, ve_sem, rstd_sem):
                pool.wait_ge(moments, tile(b, i))
                if ln < 2:
                    nc.gpsimd.tensor_tensor(neg_mean[:, ln, i:i + 1], zero[:, :], mv[:, i, 0:1], ALU.subtract)
                nc.gpsimd.tensor_tensor(ve[:, ln, i:i + 1], mv[:, i, 1:2], eps[:, :], ALU.add).then_inc(ve_sem, 1)
                pool.wait_ge(ve_sem, tile(b, i))
                nc.gpsimd.tensor_tensor(rstd[:, ln, i:i + 1], ve[:, ln, i:i + 1], neg_half[:, :],
                                        ALU.pow).then_inc(rstd_sem, 1)

            def shift(b, i, ln, rstd_sem, ln_sem):
                pool.wait_ge(rstd_sem, tile(b, i))
                nc.gpsimd.tensor_tensor(nmr[:, ln, i:i + 1], neg_mean[:, ln, i:i + 1], rstd[:, ln, i:i + 1],
                                        ALU.mult).then_inc(ln_sem, 1)

            def ln_x(b, i):
                inverse_std(b, i, 0, x_mv, x_moments, x_ve, x_rstd)
                shift(b, i, 0, x_rstd, x_ln)

            def residual(b, i):
                pool.wait_ge(h_ready, tile(b, i))
                nc.gpsimd.tensor_tensor(s_sb[:, i, :], s_sb[:, i, :], b2_sb[:, :], ALU.add).then_inc(s_biased, 1)
                pool.wait_ge(s_biased, tile(b, i))
                nc.gpsimd.tensor_tensor(s_sb[:, i, :], s_sb[:, i, :], h_sb[:, i % 2, :], ALU.add).then_inc(s_ready, 1)

            def graph(b, more):
                for i in range(NT):
                    inverse_std(b, i, 1, x1_mv, x1_moments, x1_ve, x1_rstd)
                    shift(b, i, 1, x1_rstd, x1_ln)
                    if i >= 1:
                        residual(b, i - 1)
                residual(b, NT - 1)
                for i in range(NT + T_LAG + 1):
                    if i < NT:
                        inverse_std(b, i, 2, t_mv, t_moments, t_ve, t_rstd)
                    if more and i > T_LAG:
                        ln_x(b + 1, i - T_LAG - 1)

            nc.gpsimd.memset(zero[:, :], 0.0).then_inc(consts_set, 1)
            nc.gpsimd.memset(eps[:, :], LN_EPS).then_inc(consts_set, 1)
            nc.gpsimd.memset(neg_half[:, :], -0.5).then_inc(consts_set, 1)
            pool.wait_ge(consts_set, 3)
            for i in range(NT):
                ln_x(0, i)
            pool.wait_ge(rows_loaded, 4 * DMA)
            with pool.Fori(0, B - 1) as b:
                graph(b, True)
            graph(B - 1, False)

        @block.vector
        def _(dve):
            def stats_x(b, i):
                dve.wait_ge(x_loaded[i * X_PARTS // NT], b * DMA + DMA)
                nc.vector.bn_stats(x_st[:, i, :], x_sb[:, i, :]).then_inc(x_stats, 1)

            def moments_x(i):
                nc.vector.bn_aggr(x_mv[:, i, :], x_st[:, i, :]).then_inc(x_moments, 1)

            def mask_rows(b, i):
                dve.wait_ge(adj_loaded[i % SLOTS], loaded(b, i))
                if i == 0:
                    dve.wait_ge(wrow_loaded, b * DMA + DMA)
                slot = adj_in[:, i % SLOTS, :]
                nc.vector.tensor_scalar(H[:, i, :], slot, 0.0, None, ALU.not_equal).then_inc(H_set, 1)
                dve.wait_ge(H_set, tile(b, i))
                nc.vector.scalar_tensor_tensor(out=slot, in0=slot, scalar=0.0, in1=wrow[:, :], op0=ALU.not_equal,
                                               op1=ALU.mult, accum_out=d_sum[:, i:i + 1]).then_inc(adj_used, 1)

            def invert_d(b):
                dve.wait_ge(adj_used, tile(b, NT - 1))
                nc.vector.tensor_scalar(d_pos[:, :], d_sum[:, :], 0.0, None, ALU.is_gt).then_inc(d_positive, 1)
                nc.vector.tensor_scalar(d_safe[:, :], d_sum[:, :], TINY, None, ALU.max).then_inc(d_guarded, 1)
                dve.wait_ge(d_guarded, b + 1)
                nc.vector.reciprocal(d_rec[:, :], d_safe[:, :]).then_inc(d_divided, 1)
                dve.wait_ge(d_divided, b + 1)
                nc.vector.tensor_tensor(d_inv[:, :], d_rec[:, :], d_pos[:, :], ALU.mult).then_inc(d_ready, 1)

            def split_h(b, i):
                dve.wait_ge(h_ready, tile(b, i))
                nc.vector.tensor_tensor(v_lo[:, i, :], h_sb[:, i % 2, :], v_hi[:, i, 0:F].bitcast(F32),
                                        ALU.subtract).then_inc(h_split, 1)

            def guard_count(b, e):
                dve.wait_ge(acc_full, full(b, "C1", e))
                nc.vector.tensor_scalar(cnt[:, e:e + 1], acc("C1", e)[:, F:F + 1], 1.0, None,
                                        ALU.max).then_inc(cnt_guarded, 1)

            def invert_count(b, e):
                dve.wait_ge(cnt_guarded, tile(b, e))
                nc.vector.reciprocal(b_inv[:, e:e + 1], cnt[:, e:e + 1]).then_inc(b_ready, 1)

            def split_g(key, e, parts):
                dve.wait_ge(g_hi_ready, parts)
                nc.vector.scalar_tensor_tensor(out=g_lo[:, e, :], in0=acc(key, e)[:, 0:F], scalar=b_inv[:, e:e + 1],
                                               in1=g_hi[:, e, :].bitcast(F32), op0=ALU.mult,
                                               op1=ALU.subtract).then_inc(acc_drained, 1)

            def graph(b, more):
                for i in range(NT):
                    dve.wait_ge(acc_full, full(b, "Z", i))
                    dve.wait_ge(za_ready, tile(b, i))
                    nc.vector.tensor_copy(zb[:, i, 0:F], acc("Z", i)[:, F:2 * F]).then_inc(acc_drained, 1)
                    if i % 2 == 0:
                        mask_rows(b, NT // 2 + i // 2)
                invert_d(b)
                for i in range(NT):
                    ps = acc("A", i)
                    dve.wait_ge(acc_full, full(b, "A", i))
                    nc.vector.tensor_scalar(deg[:, i:i + 1], ps[:, F:F + 1], DEG_EPS, None,
                                            ALU.max).then_inc(deg_guarded, 1)
                    dve.wait_ge(deg_guarded, tile(b, i))
                    nc.vector.reciprocal(deg_inv[:, i:i + 1], deg[:, i:i + 1]).then_inc(deg_divided, 1)
                    dve.wait_ge(deg_divided, tile(b, i))
                    nc.vector.scalar_tensor_tensor(out=u_sb[:, i % 2, :], in0=ps[:, 0:F], scalar=deg_inv[:, i:i + 1],
                                                   in1=za[:, i, :], op0=ALU.mult, op1=ALU.add).then_inc(acc_drained, 1)
                    dve.wait_ge(acc_drained, drained(b, "A", i))
                    if i == 0:
                        dve.wait_ge(out_stored, b * (DMA * NT) + DMA)
                    nc.vector.scalar_tensor_tensor(out=s_sb[:, i, :], in0=u_sb[:, i % 2, :], scalar=0.0,
                                                   in1=x_sb[:, i, :], op0=ALU.max, op1=ALU.add).then_inc(x1_ready, 1)
                    dve.wait_ge(x1_ready, tile(b, i))
                    nc.vector.bn_stats(x1_st[:, i, :], s_sb[:, i, :]).then_inc(x1_stats, 1)
                    dve.wait_ge(ones_set, 3)
                    dve.wait_ge(x1_stats, tile(b, i))
                    nc.vector.bn_aggr(x1_mv[:, i, :], x1_st[:, i, :]).then_inc(x1_moments, 1)
                    if i >= 1:
                        split_h(b, i - 1)
                    dve.wait_ge(adjT_loaded[i % SLOTS], loaded(b, i))
                    nc.vector.tensor_scalar(HT[:, :, i * P:(i + 1) * P], adjT_in[:, i % SLOTS, :, :], 0.0, None,
                                            ALU.not_equal).then_inc(adjT_used, 1)
                split_h(b, NT - 1)
                guard_count(b, 0)
                invert_count(b, 0)
                for e in range(NT):
                    ahead = e + 1 < ACC_BANKS
                    if ahead:
                        guard_count(b, e + 1)
                    if e >= ACC_BANKS:
                        guard_count(b, e)
                        invert_count(b, e)
                    dve.wait_ge(b_ready, tile(b, e))
                    split_g("C1", e, b * (2 * NT) + (e + 1))
                    if ahead:
                        invert_count(b, e + 1)
                for c in range(CH):
                    for f in range(FT):
                        n = c * FT + f
                        dve.wait_ge(acc_full, full(b, "C2", n))
                        nc.vector.tensor_copy(uT[:, f, c * 512:(c + 1) * 512], acc("C2", n)[:, :]).then_inc(acc_drained, 1)
                dve.wait_ge(rows_loaded, 4 * DMA)
                dve.wait_ge(d_ready, b + 1)
                for i in range(NT + T_LAG + 1):
                    if i < NT:
                        dve.wait_ge(acc_full, full(b, "W1", i))
                        nc.vector.scalar_tensor_tensor(out=v1_sb[:, :], in0=acc("W1", i)[:, :], scalar=d_inv[:, i:i + 1],
                                                       in1=b1_sb[:, :], op0=ALU.mult,
                                                       op1=ALU.add).then_inc(acc_drained, 1)
                    if 1 <= i <= NT:
                        j = i - 1
                        dve.wait_ge(t_rstd, tile(b, j))
                        nc.vector.tensor_scalar(t_sb[:, j % (T_LAG + 1), :], t_sb[:, j % (T_LAG + 1), :], t_mv[:, j, 0:1],
                                                rstd[:, 2, j:j + 1], ALU.subtract, ALU.mult).then_inc(n_ready, 1)
                    if i < NT:
                        dve.wait_ge(acc_drained, drained(b, "W1", i))
                        if i > T_LAG:
                            dve.wait_ge(tp_full, hn_group(b, i - T_LAG - 1) + 1)
                        nc.vector.tensor_scalar(t_sb[:, i % (T_LAG + 1), :], v1_sb[:, :], 0.0, None, ALU.max).then_inc(t_ready, 1)
                        dve.wait_ge(t_ready, tile(b, i))
                        nc.vector.bn_stats(t_st[:, i, :], t_sb[:, i % (T_LAG + 1), :]).then_inc(t_stats, 1)
                        dve.wait_ge(ones_set, 3)
                        dve.wait_ge(t_stats, tile(b, i))
                        nc.vector.bn_aggr(t_mv[:, i, :], t_st[:, i, :]).then_inc(t_moments, 1)
                    if i > T_LAG:
                        j = i - T_LAG - 1
                        if more:
                            stats_x(b + 1, j)
                            dve.wait_ge(x_stats, tile(b + 1, j))
                        dve.wait_ge(y_hi_ready, tile(b, j))
                        nc.vector.tensor_tensor(v_lo[:, j, :], acc("W2", j)[:, 0:F], v_hi[:, j, 0:F].bitcast(F32),
                                                ALU.subtract).then_inc(acc_drained, 1)
                        if more:
                            moments_x(j)
                for e in range(NT):
                    split_g("C3", e, b * (2 * NT) + (NT + e + 1))
                for i in range(NT):
                    dve.wait_ge(acc_full, full(b, "C4", i))
                    dve.wait_ge(s_ready, tile(b, i))
                    nc.vector.scalar_tensor_tensor(out=s_sb[:, i, :], in0=acc("C4", i)[:, 0:F], scalar=d_inv[:, i:i + 1],
                                                   in1=s_sb[:, i, :], op0=ALU.mult, op1=ALU.add).then_inc(acc_drained, 1)
                    if more and i % 2 == 0:
                        mask_rows(b + 1, i // 2)

            nc.vector.memset(zb[:, :, F:F + 1], 1.0).then_inc(ones_set, 1)
            nc.vector.memset(v_hi[:, :, F:F + 1].bitcast(F32), 1.0).then_inc(ones_set, 1)
            nc.vector.memset(v_hi[:, :, F + 1:F + 2].bitcast(F32), 0.0).then_inc(ones_set, 1)
            dve.sem_inc(acc_drained, ACC_BANKS)
            for i in range(NT):
                stats_x(0, i)
                dve.wait_ge(x_stats, tile(0, i))
                moments_x(i)
            for i in range(NT // 2):
                mask_rows(0, i)
            with dve.Fori(0, B - 1) as b:
                graph(b, True)
            graph(B - 1, False)


def kernel(x, adj, L0_gnn_W, L1_gnn_W1, L1_gnn_b1, L1_gnn_gamma, L1_gnn_beta, L1_gnn_W2, L1_gnn_b2):
    import numpy as np
    import concourse.bacc as bacc
    from concourse.bass_utils import run_bass_kernel_spmd

    x, adj = np.ascontiguousarray(x), np.ascontiguousarray(adj)
    B, N, _ = adj.shape
    F = x.shape[2]
    NT = N // P

    def rows_on_partitions(a):
        a = np.asarray(a)
        return np.ascontiguousarray(a.reshape(-1, P, a.shape[1]).transpose(1, 0, 2))

    def spread(v):
        return np.ascontiguousarray(np.broadcast_to(np.asarray(v), (P, len(v))))

    def per_partition(v):
        return np.ascontiguousarray(np.asarray(v).reshape(-1, P).T)

    W = np.asarray(L0_gnn_W)
    arrays = {
        "x": x,
        "adj": adj,
        "adj_t": np.ascontiguousarray(adj.reshape(B, NT, P, NT, P).transpose(0, 1, 4, 3, 2)),
        "w0": rows_on_partitions(np.concatenate([W[:, :F].T, W[:, F:].T], axis=1)),
        "w1": rows_on_partitions(np.asarray(L1_gnn_W1).T),
        "w2": rows_on_partitions(np.asarray(L1_gnn_W2).T),
        "b1": spread(L1_gnn_b1),
        "b2": spread(L1_gnn_b2),
        "gamma": per_partition(L1_gnn_gamma),
        "beta": per_partition(L1_gnn_beta),
        "ident": np.eye(P, dtype=np.float32),
    }
    nc = bacc.Bacc("TRN2", target_bir_lowering=False, num_devices=1)
    args = [nc.dram_tensor(f"in_{k}", a.shape, mybir.dt.from_np(a.dtype), kind="ExternalInput").ap()
            for k, a in arrays.items()]
    out = nc.dram_tensor("out", x.shape, F32, kind="ExternalOutput").ap()
    build(nc, *args, out)
    r = run_bass_kernel_spmd(nc, [{f"in_{k}": a for k, a in arrays.items()}], core_ids=[0])
    return r.results[0]["out"]
```

```python
from contextlib import ExitStack

import concourse.bass as bass
from concourse import mybir
from concourse.alu_op_type import AluOpType as ALU


F32 = mybir.dt.float32
F32R = mybir.dt.float32r
ACT = mybir.ActivationFunctionType

P = 128
ACC_BANKS = 6
TP_BANKS = 2
SLOTS = 4
X_PARTS = 4
T_LAG = 3
FIRST = 5
Z_MASKS = (1, 4)
A_MASKS = (1, 3)
DEG_EPS = 1e-6
LN_EPS = 1e-5
TINY = 1.1754944e-38
DMA = 16


def acc_order(NT, chunks, FT):
    order = [("Z", i) for i in range(NT)] + [("A", i) for i in range(NT)] + [("C1", i) for i in range(NT)]
    order += [("C2", c * FT + f) for c in range(chunks) for f in range(FT)]
    for i in range(NT + T_LAG + 1):
        if i < NT:
            order.append(("W1", i))
        if i > T_LAG:
            order.append(("W2", i - T_LAG - 1))
    order += [("C3", i) for i in range(NT)] + [("C4", i) for i in range(NT)]
    return {key: n for n, key in enumerate(order)}


def build(nc, x, x_t, adj, adj_t, w0, w1, w2, b1, b2, gamma, beta, ident, means, out):
    B, N, _ = adj.shape
    F = x.shape[2]
    D = w1.shape[2]
    NT = N // P
    FT = F // P
    DT = D // P
    CH = N // 512
    NUM = acc_order(NT, CH, FT)
    PER = len(NUM)
    PAIRS = NT // 2
    assert PER % ACC_BANKS == 0 and PAIRS % TP_BANKS == 0 and 4 * F <= 1024 and NT % SLOTS == 0 and D == 512

    with ExitStack() as ctx:
        def sb(name, shape, dt=F32):
            return ctx.enter_context(nc.sbuf_tensor(name, shape, dt))

        def sem(name):
            return ctx.enter_context(nc.semaphore(name))

        adj_in = sb("adj_in", [P, SLOTS, N])
        adjT_in = sb("adjT_in", [P, SLOTS, NT, P])
        H = sb("H", [P, NT, N], F32R)
        HT = sb("HT", [P, NT, N], F32R)
        x_sb = sb("x_sb", [P, NT, F])
        s_sb = sb("s_sb", [P, NT, F])
        fbuf = sb("fbuf", [P, NT * F])
        zb = sb("zb", [P, NT, F + 1])
        v_sb = sb("v_sb", [P, NT, 2, F], F32R)
        g_sb = sb("g_sb", [P, NT, 2, F], F32R)
        w0_sb = sb("w0_sb", [P, FT, 2 * F])
        w1_sb = sb("w1_sb", [P, FT, D])
        w2_sb = sb("w2_sb", [P, DT, F])
        b1_sb = sb("b1_sb", [P, D])
        b2_sb = sb("b2_sb", [P, F])
        gamma_sb = sb("gamma_sb", [P, DT])
        beta_sb = sb("beta_sb", [P, DT])
        ident_sb = sb("ident_sb", [P, P])
        wrow = sb("wrow", [P, N])
        mean_row = sb("mean_row", [P, P, NT])
        u_sb = sb("u_sb", [P, F])
        h_sb = sb("h_sb", [P, 2, F])
        low_sb = sb("low_sb", [P, 2, F])
        sum_sb = sb("sum_sb", [P, 3, F])
        v1_sb = sb("v1_sb", [P, D])
        t_sb = sb("t_sb", [P, T_LAG + 1, D])
        hnT = sb("hnT", [P, 2, DT, P])
        neg_half = sb("neg_half", [P, 1])
        zero = sb("zero", [P, 1])
        eps = sb("eps", [P, 1])
        neg_mean = sb("neg_mean", [P, NT])
        x_st = sb("x_st", [P, NT, 6])
        x_mv = sb("x_mv", [P, NT, 2])
        x_mean = sb("x_mean", [P, NT])
        x1_st = sb("x1_st", [P, NT, 6])
        x1_mv = sb("x1_mv", [P, NT, 2])
        t_st = sb("t_st", [P, NT, 6])
        t_mv = sb("t_mv", [P, NT, 2])
        ve = sb("ve", [P, 3, NT])
        rstd = sb("rstd", [P, 3, NT])
        nmr = sb("nmr", [P, NT])
        deg = sb("deg", [P, NT])
        deg_inv = sb("deg_inv", [P, NT])
        cnt_half = sb("cnt_half", [P, 2, NT])
        cnt_sum = sb("cnt_sum", [P, NT])
        cnt = sb("cnt", [P, NT])
        b_inv = sb("b_inv", [P, NT])
        d_sum = sb("d_sum", [P, NT])
        d_pos = sb("d_pos", [P, NT])
        d_safe = sb("d_safe", [P, NT])
        d_rec = sb("d_rec", [P, NT])
        d_inv = sb("d_inv", [P, NT])

        cT = fbuf[:, :].rearrange("p (i f n) -> p i f n", i=NT, f=FT)
        za = fbuf[:, :].rearrange("p (i f) -> p i f", i=NT)
        uT = fbuf[:, :].rearrange("p (f n) -> p f n", f=FT)
        c0 = t_sb[:, :, :].rearrange("p a (b f) -> p (a b) f", f=F)

        acc_banks = [ctx.enter_context(nc.psum_tensor(f"acc{k}", [P, 512], F32)) for k in range(ACC_BANKS)]
        tp_banks = [ctx.enter_context(nc.psum_tensor(f"tp{k}", [P, 512], F32)) for k in range(TP_BANKS)]

        def acc(key, i):
            return acc_banks[NUM[key, i] % ACC_BANKS]

        adj_loaded = [sem(f"adj_loaded{k}") for k in range(SLOTS)]
        adjT_loaded = [sem(f"adjT_loaded{k}") for k in range(SLOTS)]
        x_loaded = [sem(f"x_loaded{k}") for k in range(X_PARTS)]
        wrow_loaded = sem("wrow_loaded")
        ident_loaded = sem("ident_loaded")
        w0_loaded = sem("w0_loaded")
        w12_loaded = sem("w12_loaded")
        rows_loaded = sem("rows_loaded")
        out_stored = sem("out_stored")
        acc_full = sem("acc_full")
        acc_drained = sem("acc_drained")
        tp_full = sem("tp_full")
        tp_drained = sem("tp_drained")
        ones_set = sem("ones_set")
        consts_set = sem("consts_set")
        x_stats = sem("x_stats")
        x_moments = sem("x_moments")
        x_ve = sem("x_ve")
        x_rstd = sem("x_rstd")
        x_mean_ready = sem("x_mean_ready")
        mean_stored = sem("mean_stored")
        mean_loaded = sem("mean_loaded")
        xT_loaded = sem("xT_loaded")
        x_mean_negated = sem("x_mean_negated")
        even_c_ready = sem("even_c_ready")
        odd_c_ready = sem("odd_c_ready")
        xT_centered = sem("xT_centered")
        cT_ready = sem("cT_ready")
        H_set = sem("H_set")
        adj_used = sem("adj_used")
        d_positive = sem("d_positive")
        d_guarded = sem("d_guarded")
        d_divided = sem("d_divided")
        d_ready = sem("d_ready")
        za_ready = sem("za_ready")
        deg_guarded = sem("deg_guarded")
        deg_divided = sem("deg_divided")
        x1_ready = sem("x1_ready")
        x1_stats = sem("x1_stats")
        x1_moments = sem("x1_moments")
        x1_ve = sem("x1_ve")
        x1_rstd = sem("x1_rstd")
        x1_ln = sem("x1_ln")
        h_ready = sem("h_ready")
        h_split = sem("h_split")
        s_biased = sem("s_biased")
        s_ready = sem("s_ready")
        adjT_used = sem("adjT_used")
        half_counted = sem("half_counted")
        rest_counted = sem("rest_counted")
        cnt_summed = sem("cnt_summed")
        cnt_guarded = sem("cnt_guarded")
        b_ready = sem("b_ready")
        low_scaled = sem("low_scaled")
        g_hi_ready = sem("g_hi_ready")
        g_ready = sem("g_ready")
        out_ready = sem("out_ready")
        t_ready = sem("t_ready")
        t_stats = sem("t_stats")
        t_moments = sem("t_moments")
        t_ve = sem("t_ve")
        t_rstd = sem("t_rstd")
        n_ready = sem("n_ready")
        y_hi_ready = sem("y_hi_ready")

        def tile(b, i):
            return b * NT + (i + 1)

        def full(b, key, i):
            return b * PER + (NUM[key, i] + 1)

        def drained(b, key, i):
            return b * PER + (NUM[key, i] + 1 + ACC_BANKS)

        def bank_free(b, key, i):
            return b * PER + (NUM[key, i] + 1)

        def hn_group(b, i):
            return b * NT + (PAIRS + i)

        def pair(b, q):
            return b * PAIRS + (q + 1)

        def g_tile(b, key, e):
            return b * (2 * NT) + ((NT if key == "C3" else 0) + e + 1)

        def low_tile(b, key, i):
            return b * (3 * NT) + ({"C1": 0, "C3": NT, "C4": 2 * NT}[key] + i + 1)

        COUNTS = NT + NT // 2

        def loaded(b, i):
            return b * (DMA * NT // SLOTS) + DMA * (i // SLOTS + 1)

        block = ctx.enter_context(nc.Block())

        @block.sync
        def _(sp):
            def load_adj(b, i):
                sp.dma_start(adj_in[:, i % SLOTS, :], adj[b, i * P:(i + 1) * P, :]).then_inc(adj_loaded[i % SLOTS], DMA)

            def load_adjT(b, i):
                sp.dma_start(adjT_in[:, i % SLOTS, :, :], adj_t[b, i]).then_inc(adjT_loaded[i % SLOTS], DMA)

            def load_x(b, parts=range(X_PARTS)):
                w = NT // X_PARTS
                for k in parts:
                    part = x[b, k * w * P:(k + 1) * w * P, :].rearrange("(i p) f -> p i f", p=P)
                    sp.dma_start(x_sb[:, k * w:(k + 1) * w, :], part).then_inc(x_loaded[k], DMA)

            def load_wrow(b):
                sp.dma_start(wrow[:, :], adj[b, 0:1, :].to_broadcast([P, N])).then_inc(wrow_loaded, DMA)

            sp.sem_inc(out_stored, DMA)
            load_x(0, (0,))
            sp.dma_start(ident_sb[:, :], ident).then_inc(ident_loaded, DMA)
            load_x(0, range(1, X_PARTS))
            sp.dma_start(w0_sb[:, :, :], w0).then_inc(w0_loaded, DMA)
            load_wrow(0)
            for i in range(SLOTS):
                load_adj(0, i)
            for i in range(SLOTS):
                load_adjT(0, i)
                sp.wait_ge(adj_used, tile(0, i))
                load_adj(0, SLOTS + i)
            for dst, src in ((b1_sb, b1), (b2_sb, b2), (gamma_sb, gamma), (beta_sb, beta)):
                sp.dma_start(dst[:, :], src).then_inc(rows_loaded, DMA)
            for dst, src in ((w1_sb, w1), (w2_sb, w2)):
                sp.dma_start(dst[:, :, :], src).then_inc(w12_loaded, DMA)

            def graph(b, more):
                for i in range(SLOTS, NT):
                    sp.wait_ge(adjT_used, tile(b, i - SLOTS))
                    load_adjT(b, i)
                if more:
                    for i in range(SLOTS):
                        sp.wait_ge(adj_used, tile(b, NT - SLOTS + i))
                        load_adj(b + 1, i)
                    load_wrow(b + 1)
                    for i in range(SLOTS):
                        sp.wait_ge(adjT_used, tile(b, NT - SLOTS + i))
                        load_adjT(b + 1, i)
                    sp.wait_ge(x1_ready, tile(b, NT - 1))
                    load_x(b + 1)
                    sp.wait_ge(acc_full, full(b, "W1", NT - 1))
                    sp.dma_start(fbuf[:, :], x_t[b + 1]).then_inc(xT_loaded, DMA)
                    sp.wait_ge(x_mean_ready, tile(b + 1, NT - 1) - NT)
                    sp.dma_start(means, x_mean[:, :]).then_inc(mean_stored, DMA)
                    sp.wait_ge(mean_stored, b * DMA + DMA)
                    sp.dma_start(mean_row[:, :, :], means.rearrange("(o n) i -> o n i", o=1).to_broadcast([P, P, NT])
                                 ).then_inc(mean_loaded, DMA)
                for i in range(NT):
                    sp.wait_ge(out_ready, tile(b, i))
                    sp.dma_start(out[b, i * P:(i + 1) * P, :], s_sb[:, i, :]).then_inc(out_stored, DMA)
                    if more and i % 2 == 1:
                        sp.wait_ge(adj_used, tile(b + 1, i // 2))
                        load_adj(b + 1, SLOTS + i // 2)

            with sp.Fori(0, B - 1) as b:
                graph(b, True)
            graph(B - 1, False)
            sp.wait_ge(out_stored, DMA * (B * NT + 1))

        @block.tensor
        def _(pe):
            def take_bank(b, key, i):
                pe.wait_ge(acc_drained, bank_free(b, key, i))

            def transpose_c0(q):
                pe.wait_ge(tp_drained, q + 1)
                for i in (2 * q, 2 * q + 1):
                    pe.wait_ge(odd_c_ready if i % 2 else even_c_ready, q + 1)
                    for f in range(FT):
                        piece = ((i % 2) * FT + f) * P
                        last = nc.tensor.transpose(tp_banks[q % TP_BANKS][:, piece:piece + P],
                                                   c0[:, i, f * P:(f + 1) * P], ident_sb[:, :])
                last.then_inc(tp_full, 1)

            def step(key, t, k):
                lhs, rhs = (HT, g_sb) if key == "C4" else (H, v_sb)
                last = nc.tensor.matmul(acc(key, t)[:, :], lhs[:, k, t * P:(t + 1) * P], rhs[:, k, :, :],
                                        start=(k == 0), stop=(k == NT - 1))
                if k == NT - 1:
                    last.then_inc(acc_full, 1)

            def first_tiles(b, key, tiles, early, sem_, count):
                for t in range(tiles):
                    take_bank(b, key, t)
                    for k in range(early):
                        if t == 0:
                            pe.wait_ge(sem_, count(k))
                        step(key, t, k)
                for t in range(tiles):
                    for k in range(early, NT):
                        if t == 0:
                            pe.wait_ge(sem_, count(k))
                        step(key, t, k)

            def graph(b, more):
                for i in range(NT):
                    take_bank(b, "Z", i)
                    if i % 2 == 0:
                        pe.wait_ge(cT_ready, pair(b, i // 2))
                    for f in range(FT):
                        last = nc.tensor.matmul(acc("Z", i)[:, :], cT[:, i, f, :], w0_sb[:, f, :],
                                                start=(f == 0), stop=(f == FT - 1))
                    last.then_inc(acc_full, 1)
                for i in range(NT):
                    take_bank(b, "A", i)
                    pe.wait_ge(adjT_loaded[i % SLOTS], loaded(b, i))
                    for k in range(NT):
                        if i == 0:
                            pe.wait_ge(acc_drained, drained(b, "Z", k))
                        last = nc.tensor.matmul(acc("A", i)[:, 0:F + 1], adjT_in[:, i % SLOTS, k, :], zb[:, k, :],
                                                start=(k == 0), stop=(k == NT - 1))
                    last.then_inc(acc_full, 1)
                pe.wait_ge(H_set, tile(b, NT - 1))
                first_tiles(b, "C1", FIRST, NT - 2, h_split, lambda k: tile(b, k))
                for e in range(FIRST, NT):
                    take_bank(b, "C1", e)
                    for k in range(NT):
                        step("C1", e, k)
                pe.wait_ge(adjT_used, tile(b, NT - 1))
                for c in range(CH):
                    for f in range(FT):
                        n = c * FT + f
                        take_bank(b, "C2", n)
                        for k in range(NT):
                            if n == 0:
                                pe.wait_ge(g_ready, g_tile(b, "C1", k))
                            rhs = HT[:, k, c * 512:(c + 1) * 512]
                            nc.tensor.matmul(acc("C2", n)[:, :], g_sb[:, k, 0, f * P:(f + 1) * P], rhs,
                                             start=(k == 0), stop=False)
                            last = nc.tensor.matmul(acc("C2", n)[:, :], g_sb[:, k, 1, f * P:(f + 1) * P], rhs,
                                                    start=False, stop=(k == NT - 1))
                        last.then_inc(acc_full, 1)
                pe.wait_ge(w12_loaded, 2 * DMA)
                for i in range(NT + T_LAG + 1):
                    if i < NT:
                        take_bank(b, "W1", i)
                        pe.wait_ge(acc_drained, drained(b, "C2", (i * P // 512) * FT + FT - 1))
                        for f in range(FT):
                            last = nc.tensor.matmul(acc("W1", i)[:, :], uT[:, f, i * P:(i + 1) * P], w1_sb[:, f, :],
                                                    start=(f == 0), stop=(f == FT - 1))
                        last.then_inc(acc_full, 1)
                    if T_LAG <= i < NT + T_LAG:
                        j = i - T_LAG
                        pe.wait_ge(tp_drained, hn_group(b, j) + 1)
                        pe.wait_ge(n_ready, tile(b, j))
                        for d in range(DT):
                            last = nc.tensor.transpose(tp_banks[j % TP_BANKS][:, d * P:(d + 1) * P],
                                                       t_sb[:, j % (T_LAG + 1), d * P:(d + 1) * P], ident_sb[:, :])
                        last.then_inc(tp_full, 1)
                    if i > T_LAG:
                        j = i - T_LAG - 1
                        take_bank(b, "W2", j)
                        pe.wait_ge(tp_drained, hn_group(b, j) + 1 + TP_BANKS)
                        for d in range(DT):
                            last = nc.tensor.matmul(acc("W2", j)[:, 0:F], hnT[:, j % 2, d, :], w2_sb[:, d, :],
                                                    start=(d == 0), stop=(d == DT - 1))
                        last.then_inc(acc_full, 1)
                first_tiles(b, "C3", 2, NT - 1, acc_drained, lambda k: drained(b, "W2", k))
                for e in range(2, NT):
                    take_bank(b, "C3", e)
                    for k in range(NT):
                        step("C3", e, k)
                first_tiles(b, "C4", 3, NT - 2, g_ready, lambda k: g_tile(b, "C3", k))
                for i in range(3, NT):
                    take_bank(b, "C4", i)
                    for k in range(NT):
                        step("C4", i, k)

            pe.wait_ge(ident_loaded, DMA)
            for q in range(PAIRS):
                transpose_c0(q)
            pe.wait_ge(w0_loaded, DMA)
            pe.wait_ge(ones_set, 1)
            with pe.Fori(0, B - 1) as b:
                graph(b, True)
            graph(B - 1, False)

        @block.scalar
        def _(act):
            def make_cT(b, q):
                act.wait_ge(xT_centered, (b - 1) * PAIRS + (q + 1))
                nc.scalar.activation(cT[:, 2 * q:2 * q + 2, :, :], cT[:, 2 * q:2 * q + 2, :, :],
                                     ACT.Relu).then_inc(cT_ready, 1)

            def count(b, n, e, half):
                act.wait_ge(adjT_used, tile(b, (half + 1) * NT // 2 - 1))
                if n >= 4:
                    act.wait_ge(half_counted, b * COUNTS + (n - 3))
                nc.scalar.activation(t_sb[:, n % 4, :], HT[:, e, half * N // 2:(half + 1) * N // 2].bitcast(F32),
                                     ACT.Copy, accum_out=cnt_half[:, half, e:e + 1]).then_inc(half_counted, 1)

            def scale_low(b, key, i, scales):
                act.wait_ge(acc_full, full(b, key, i))
                if i >= 2:
                    act.wait_ge(acc_drained, drained(b, key, i - 2))
                nc.scalar.activation(low_sb[:, i % 2, :], acc(key, i)[:, F:2 * F], ACT.Copy,
                                     scale=scales[:, i:i + 1]).then_inc(low_scaled, 1)

            def make_g_hi(b, key, e):
                act.wait_ge(acc_drained, drained(b, key, e))
                nc.scalar.activation(g_sb[:, e, 0, :], sum_sb[:, e % 3, :], ACT.Copy).then_inc(g_hi_ready, 1)

            def graph(b, more):
                for i in range(NT):
                    act.wait_ge(acc_full, full(b, "Z", i))
                    act.wait_ge(x_rstd, tile(b, i))
                    nc.scalar.activation(za[:, i, :], acc("Z", i)[:, 0:F], ACT.Copy,
                                         scale=rstd[:, 0, i:i + 1]).then_inc(za_ready, 1)
                for i in range(NT):
                    act.wait_ge(x1_ln, tile(b, i))
                    if i >= 2:
                        act.wait_ge(h_split, tile(b, i - 2))
                        act.wait_ge(s_ready, tile(b, i - 2))
                    nc.scalar.activation(h_sb[:, i % 2, :], s_sb[:, i, :], ACT.Relu, bias=nmr[:, i:i + 1],
                                         scale=rstd[:, 1, i:i + 1])
                    nc.scalar.activation(v_sb[:, i, 0, :], s_sb[:, i, :], ACT.Relu, bias=nmr[:, i:i + 1],
                                         scale=rstd[:, 1, i:i + 1]).then_inc(h_ready, 1)
                    if i >= NT // 2:
                        for n in (2 * i - NT, 2 * i - NT + 1):
                            count(b, n, n, 0)
                for n in range(NT, COUNTS):
                    count(b, n, n - NT // 2, 1)
                act.wait_ge(b_ready, b + 1)
                for e in range(NT + 1):
                    if e < NT:
                        scale_low(b, "C1", e, b_inv)
                    if e >= 1:
                        make_g_hi(b, "C1", e - 1)
                act.wait_ge(rows_loaded, 4 * DMA)
                for i in range(T_LAG, NT + T_LAG + 1):
                    if i < NT + T_LAG:
                        j = i - T_LAG
                        act.wait_ge(tp_full, hn_group(b, j) + 1)
                        for d in range(DT):
                            last = nc.scalar.activation(hnT[:, j % 2, d, :], tp_banks[j % TP_BANKS][:, d * P:(d + 1) * P],
                                                        ACT.Identity, bias=beta_sb[:, d:d + 1],
                                                        scale=gamma_sb[:, d:d + 1])
                        last.then_inc(tp_drained, 1)
                    if i > T_LAG:
                        j = i - T_LAG - 1
                        act.wait_ge(acc_full, full(b, "W2", j))
                        nc.scalar.activation(v_sb[:, j, 0, :], acc("W2", j)[:, 0:F], ACT.Copy).then_inc(y_hi_ready, 1)
                for e in range(NT + 1):
                    if e < NT:
                        scale_low(b, "C3", e, b_inv)
                    if e >= 1:
                        make_g_hi(b, "C3", e - 1)
                for i in range(NT):
                    scale_low(b, "C4", i, d_inv)
                    if more and i < PAIRS:
                        make_cT(b + 1, i)

            act.sem_inc(tp_drained, TP_BANKS)
            def make_odd_c(q):
                i = 2 * q + 1
                act.wait_ge(x_mean_negated, q + 1)
                nc.scalar.activation(c0[:, i, :], x_sb[:, i, :], ACT.Relu, bias=x_mean[:, i:i + 1]).then_inc(odd_c_ready, 1)

            make_odd_c(0)
            for q in range(PAIRS):
                if q + 1 < PAIRS:
                    make_odd_c(q + 1)
                act.wait_ge(tp_full, q + 1)
                nc.scalar.activation(cT[:, 2 * q:2 * q + 2, :, :], tp_banks[q % TP_BANKS][:, :], ACT.Copy).then_inc(tp_drained, 1)
                act.wait_ge(tp_drained, q + 1 + TP_BANKS)
                act.sem_inc(cT_ready, 1)
            with act.Fori(0, B - 1) as b:
                graph(b, True)
            graph(B - 1, False)

        @block.gpsimd
        def _(pool):
            def inverse_std(b, i, ln, mv, moments, ve_sem, rstd_sem):
                pool.wait_ge(moments, tile(b, i))
                if ln == 1:
                    nc.gpsimd.tensor_tensor(neg_mean[:, i:i + 1], zero[:, :], mv[:, i, 0:1], ALU.subtract)
                nc.gpsimd.tensor_tensor(ve[:, ln, i:i + 1], mv[:, i, 1:2], eps[:, :], ALU.add).then_inc(ve_sem, 1)
                pool.wait_ge(ve_sem, tile(b, i))
                nc.gpsimd.tensor_tensor(rstd[:, ln, i:i + 1], ve[:, ln, i:i + 1], neg_half[:, :],
                                        ALU.pow).then_inc(rstd_sem, 1)

            def ln_x(b, i):
                inverse_std(b, i, 0, x_mv, x_moments, x_ve, x_rstd)

            def copy_mean(i):
                nc.gpsimd.tensor_tensor(x_mean[:, i:i + 1], x_mv[:, i, 0:1], zero[:, :], ALU.add).then_inc(x_mean_ready, 1)

            def ln_x1(b, i):
                inverse_std(b, i, 1, x1_mv, x1_moments, x1_ve, x1_rstd)
                pool.wait_ge(x1_rstd, tile(b, i))
                nc.gpsimd.tensor_tensor(nmr[:, i:i + 1], neg_mean[:, i:i + 1], rstd[:, 1, i:i + 1],
                                        ALU.mult).then_inc(x1_ln, 1)

            def center_xT(b, q):
                if q == 0:
                    pool.wait_ge(xT_loaded, (b - 1) * DMA + DMA)
                    pool.wait_ge(mean_loaded, (b - 1) * DMA + DMA)
                for f in range(FT):
                    part = cT[:, 2 * q:2 * q + 2, f, :]
                    last = nc.gpsimd.tensor_tensor(part, part, mean_row[:, :, 2 * q:2 * q + 2].rearrange("p n i -> p i n"),
                                                   ALU.subtract)
                last.then_inc(xT_centered, 1)

            def residual(b, i):
                pool.wait_ge(h_ready, tile(b, i))
                nc.gpsimd.tensor_tensor(s_sb[:, i, :], s_sb[:, i, :], b2_sb[:, :], ALU.add).then_inc(s_biased, 1)
                pool.wait_ge(s_biased, tile(b, i))
                nc.gpsimd.tensor_tensor(s_sb[:, i, :], s_sb[:, i, :], h_sb[:, i % 2, :], ALU.add).then_inc(s_ready, 1)

            def finish(b, i):
                pool.wait_ge(acc_drained, drained(b, "C4", i))
                nc.gpsimd.tensor_tensor(s_sb[:, i, :], s_sb[:, i, :], sum_sb[:, i % 3, :], ALU.add).then_inc(out_ready, 1)

            def graph(b, more):
                for i in range(NT):
                    ln_x1(b, i)
                    if i >= 1:
                        residual(b, i - 1)
                residual(b, NT - 1)
                for i in range(NT + T_LAG + 1):
                    if i < NT:
                        inverse_std(b, i, 2, t_mv, t_moments, t_ve, t_rstd)
                    if more and i > T_LAG:
                        ln_x(b + 1, i - T_LAG - 1)
                        copy_mean(i - T_LAG - 1)
                if more:
                    for q in range(PAIRS):
                        center_xT(b + 1, q)
                for i in range(NT):
                    finish(b, i)

            nc.gpsimd.memset(zero[:, :], 0.0).then_inc(consts_set, 1)
            nc.gpsimd.memset(eps[:, :], LN_EPS).then_inc(consts_set, 1)
            nc.gpsimd.memset(neg_half[:, :], -0.5).then_inc(consts_set, 1)
            pool.wait_ge(consts_set, 3)
            for q in range(PAIRS):
                i = 2 * q + 1
                pool.wait_ge(x_moments, i + 1)
                nc.gpsimd.tensor_tensor(x_mean[:, i:i + 1], zero[:, :], x_mv[:, i, 0:1],
                                        ALU.subtract).then_inc(x_mean_negated, 1)
            for i in range(NT):
                ln_x(0, i)
            pool.wait_ge(rows_loaded, 4 * DMA)
            with pool.Fori(0, B - 1) as b:
                graph(b, True)
            graph(B - 1, False)

        @block.vector
        def _(dve):
            def stats_x(b, i):
                dve.wait_ge(x_loaded[i * X_PARTS // NT], b * DMA + DMA)
                nc.vector.bn_stats(x_st[:, i, :], x_sb[:, i, :]).then_inc(x_stats, 1)

            def moments_x(i):
                nc.vector.bn_aggr(x_mv[:, i, :], x_st[:, i, :]).then_inc(x_moments, 1)

            def mask_rows(b, i):
                dve.wait_ge(adj_loaded[i % SLOTS], loaded(b, i))
                if i == 0:
                    dve.wait_ge(wrow_loaded, b * DMA + DMA)
                slot = adj_in[:, i % SLOTS, :]
                nc.vector.tensor_scalar(H[:, i, :], slot, 0.0, None, ALU.not_equal).then_inc(H_set, 1)
                dve.wait_ge(H_set, tile(b, i))
                nc.vector.scalar_tensor_tensor(out=slot, in0=slot, scalar=0.0, in1=wrow[:, :], op0=ALU.not_equal,
                                               op1=ALU.mult, accum_out=d_sum[:, i:i + 1]).then_inc(adj_used, 1)

            def invert_d(b):
                dve.wait_ge(adj_used, tile(b, NT - 1))
                nc.vector.tensor_scalar(d_pos[:, :], d_sum[:, :], 0.0, None, ALU.is_gt).then_inc(d_positive, 1)
                nc.vector.tensor_scalar(d_safe[:, :], d_sum[:, :], TINY, None, ALU.max).then_inc(d_guarded, 1)
                dve.wait_ge(d_guarded, b + 1)
                nc.vector.reciprocal(d_rec[:, :], d_safe[:, :]).then_inc(d_divided, 1)
                dve.wait_ge(d_divided, b + 1)
                nc.vector.tensor_tensor(d_inv[:, :], d_rec[:, :], d_pos[:, :], ALU.mult).then_inc(d_ready, 1)

            def split_h(b, i):
                dve.wait_ge(h_ready, tile(b, i))
                nc.vector.tensor_tensor(v_sb[:, i, 1, :], h_sb[:, i % 2, :], v_sb[:, i, 0, :].bitcast(F32),
                                        ALU.subtract).then_inc(h_split, 1)

            def invert_counts(b):
                dve.wait_ge(adjT_used, tile(b, NT - 1))
                nc.vector.tensor_reduce(cnt_half[:, 1, 0:NT // 2], HT[:, 0:NT // 2, N // 2:N].bitcast(F32),
                                        mybir.AxisListType.X, ALU.add).then_inc(rest_counted, 1)
                dve.wait_ge(rest_counted, b + 1)
                dve.wait_ge(half_counted, b * COUNTS + COUNTS)
                nc.vector.tensor_tensor(cnt_sum[:, :], cnt_half[:, 0, :], cnt_half[:, 1, :],
                                        ALU.add).then_inc(cnt_summed, 1)
                dve.wait_ge(cnt_summed, b + 1)
                nc.vector.tensor_scalar(cnt[:, :], cnt_sum[:, :], 1.0, None, ALU.max).then_inc(cnt_guarded, 1)
                dve.wait_ge(cnt_guarded, b + 1)
                nc.vector.reciprocal(b_inv[:, :], cnt[:, :]).then_inc(b_ready, 1)
                dve.wait_ge(b_ready, b + 1)

            def add_parts(b, key, i, scales):
                dve.wait_ge(low_scaled, low_tile(b, key, i))
                if key == "C4" and i >= 3:
                    dve.wait_ge(out_ready, tile(b, i - 3))
                nc.vector.scalar_tensor_tensor(out=sum_sb[:, i % 3, :], in0=acc(key, i)[:, 0:F],
                                               scalar=scales[:, i:i + 1], in1=low_sb[:, i % 2, :], op0=ALU.mult,
                                               op1=ALU.add).then_inc(acc_drained, 1)

            def make_g_lo(b, key, e):
                dve.wait_ge(g_hi_ready, g_tile(b, key, e))
                nc.vector.tensor_tensor(g_sb[:, e, 1, :], sum_sb[:, e % 3, :], g_sb[:, e, 0, :].bitcast(F32),
                                        ALU.subtract).then_inc(g_ready, 1)

            def make_g(b, key):
                for e in range(NT + 1):
                    if e >= 3 and e < NT:
                        dve.wait_ge(g_ready, g_tile(b, key, e - 3))
                    if e < NT:
                        add_parts(b, key, e, b_inv)
                    if e >= 1:
                        make_g_lo(b, key, e - 1)

            def graph(b, more):
                for i in range(NT):
                    dve.wait_ge(acc_full, full(b, "Z", i))
                    dve.wait_ge(za_ready, tile(b, i))
                    dve.wait_ge(x_rstd, tile(b, i))
                    nc.vector.tensor_scalar(zb[:, i, 0:F], acc("Z", i)[:, F:2 * F], rstd[:, 0, i:i + 1], None,
                                            ALU.mult).then_inc(acc_drained, 1)
                    if i in Z_MASKS:
                        mask_rows(b, NT // 2 + Z_MASKS.index(i))
                for i in range(NT):
                    ps = acc("A", i)
                    dve.wait_ge(acc_full, full(b, "A", i))
                    nc.vector.tensor_scalar(deg[:, i:i + 1], ps[:, F:F + 1], DEG_EPS, None,
                                            ALU.max).then_inc(deg_guarded, 1)
                    dve.wait_ge(deg_guarded, tile(b, i))
                    nc.vector.reciprocal(deg_inv[:, i:i + 1], deg[:, i:i + 1]).then_inc(deg_divided, 1)
                    dve.wait_ge(deg_divided, tile(b, i))
                    nc.vector.scalar_tensor_tensor(out=u_sb[:, :], in0=ps[:, 0:F], scalar=deg_inv[:, i:i + 1],
                                                   in1=za[:, i, :], op0=ALU.mult, op1=ALU.add).then_inc(acc_drained, 1)
                    dve.wait_ge(acc_drained, drained(b, "A", i))
                    if i == 0:
                        dve.wait_ge(out_stored, b * (DMA * NT) + DMA)
                    nc.vector.scalar_tensor_tensor(out=s_sb[:, i, :], in0=u_sb[:, :], scalar=0.0,
                                                   in1=x_sb[:, i, :], op0=ALU.max, op1=ALU.add).then_inc(x1_ready, 1)
                    dve.wait_ge(x1_ready, tile(b, i))
                    nc.vector.bn_stats(x1_st[:, i, :], s_sb[:, i, :]).then_inc(x1_stats, 1)
                    dve.wait_ge(ones_set, 1)
                    dve.wait_ge(x1_stats, tile(b, i))
                    nc.vector.bn_aggr(x1_mv[:, i, :], x1_st[:, i, :]).then_inc(x1_moments, 1)
                    if i >= 1:
                        split_h(b, i - 1)
                    if i in A_MASKS:
                        mask_rows(b, NT // 2 + len(Z_MASKS) + A_MASKS.index(i))
                    dve.wait_ge(adjT_loaded[i % SLOTS], loaded(b, i))
                    nc.vector.tensor_scalar(HT[:, :, i * P:(i + 1) * P], adjT_in[:, i % SLOTS, :, :], 0.0, None,
                                            ALU.not_equal).then_inc(adjT_used, 1)
                split_h(b, NT - 1)
                invert_d(b)
                invert_counts(b)
                make_g(b, "C1")
                for c in range(CH):
                    for f in range(FT):
                        n = c * FT + f
                        dve.wait_ge(acc_full, full(b, "C2", n))
                        nc.vector.tensor_copy(uT[:, f, c * 512:(c + 1) * 512], acc("C2", n)[:, :]).then_inc(acc_drained, 1)
                dve.wait_ge(rows_loaded, 4 * DMA)
                dve.wait_ge(d_ready, b + 1)
                for i in range(NT + T_LAG + 1):
                    if i < NT:
                        dve.wait_ge(acc_full, full(b, "W1", i))
                        nc.vector.scalar_tensor_tensor(out=v1_sb[:, :], in0=acc("W1", i)[:, :], scalar=d_inv[:, i:i + 1],
                                                       in1=b1_sb[:, :], op0=ALU.mult,
                                                       op1=ALU.add).then_inc(acc_drained, 1)
                    if 1 <= i <= NT:
                        j = i - 1
                        dve.wait_ge(t_rstd, tile(b, j))
                        nc.vector.tensor_scalar(t_sb[:, j % (T_LAG + 1), :], t_sb[:, j % (T_LAG + 1), :], t_mv[:, j, 0:1],
                                                rstd[:, 2, j:j + 1], ALU.subtract, ALU.mult).then_inc(n_ready, 1)
                    if i < NT:
                        dve.wait_ge(acc_drained, drained(b, "W1", i))
                        if i > T_LAG:
                            dve.wait_ge(tp_full, hn_group(b, i - T_LAG - 1) + 1)
                        nc.vector.tensor_scalar(t_sb[:, i % (T_LAG + 1), :], v1_sb[:, :], 0.0, None, ALU.max).then_inc(t_ready, 1)
                        dve.wait_ge(t_ready, tile(b, i))
                        nc.vector.bn_stats(t_st[:, i, :], t_sb[:, i % (T_LAG + 1), :]).then_inc(t_stats, 1)
                        dve.wait_ge(ones_set, 1)
                        dve.wait_ge(t_stats, tile(b, i))
                        nc.vector.bn_aggr(t_mv[:, i, :], t_st[:, i, :]).then_inc(t_moments, 1)
                    if i > T_LAG:
                        j = i - T_LAG - 1
                        if more:
                            stats_x(b + 1, j)
                            dve.wait_ge(x_stats, tile(b + 1, j))
                        dve.wait_ge(y_hi_ready, tile(b, j))
                        nc.vector.tensor_tensor(v_sb[:, j, 1, :], acc("W2", j)[:, 0:F],
                                                v_sb[:, j, 0, :].bitcast(F32), ALU.subtract).then_inc(acc_drained, 1)
                        if more:
                            moments_x(j)
                make_g(b, "C3")
                for i in range(NT):
                    if i == 0:
                        dve.wait_ge(g_ready, g_tile(b, "C3", NT - 1))
                    add_parts(b, "C4", i, d_inv)
                    if more and i % 2 == 0:
                        mask_rows(b + 1, i // 2)

            nc.vector.memset(zb[:, :, F:F + 1], 1.0).then_inc(ones_set, 1)
            dve.sem_inc(acc_drained, ACC_BANKS)
            for q in range(PAIRS):
                for i in (2 * q, 2 * q + 1):
                    stats_x(0, i)
                for i in (2 * q, 2 * q + 1):
                    dve.wait_ge(x_stats, tile(0, i))
                    moments_x(i)
                i = 2 * q
                dve.wait_ge(x_moments, tile(0, i))
                nc.vector.tensor_scalar(c0[:, i, :], x_sb[:, i, :], x_mv[:, i, 0:1], 0.0, ALU.subtract,
                                        ALU.max).then_inc(even_c_ready, 1)
            for i in range(NT // 2):
                mask_rows(0, i)
            with dve.Fori(0, B - 1) as b:
                graph(b, True)
            graph(B - 1, False)


def kernel(x, adj, L0_gnn_W, L1_gnn_W1, L1_gnn_b1, L1_gnn_gamma, L1_gnn_beta, L1_gnn_W2, L1_gnn_b2):
    import numpy as np
    import concourse.bacc as bacc
    from concourse.bass_utils import run_bass_kernel_spmd

    x, adj = np.ascontiguousarray(x), np.ascontiguousarray(adj)
    B, N, _ = adj.shape
    F = x.shape[2]
    NT = N // P

    def rows_on_partitions(a):
        a = np.asarray(a)
        return np.ascontiguousarray(a.reshape(-1, P, a.shape[1]).transpose(1, 0, 2))

    def spread(v):
        return np.ascontiguousarray(np.broadcast_to(np.asarray(v), (P, len(v))))

    def per_partition(v):
        return np.ascontiguousarray(np.asarray(v).reshape(-1, P).T)

    W = np.asarray(L0_gnn_W)
    arrays = {
        "x": x,
        "x_t": np.ascontiguousarray(x.reshape(B, NT, P, F // P, P).transpose(0, 4, 1, 3, 2)).reshape(B, P, NT * F),
        "adj": adj,
        "adj_t": np.ascontiguousarray(adj.reshape(B, NT, P, NT, P).transpose(0, 1, 4, 3, 2)),
        "w0": rows_on_partitions(np.concatenate([W[:, :F].T, W[:, F:].T], axis=1)),
        "w1": rows_on_partitions(np.asarray(L1_gnn_W1).T),
        "w2": rows_on_partitions(np.asarray(L1_gnn_W2).T),
        "b1": spread(L1_gnn_b1),
        "b2": spread(L1_gnn_b2),
        "gamma": per_partition(L1_gnn_gamma),
        "beta": per_partition(L1_gnn_beta),
        "ident": np.eye(P, dtype=np.float32),
    }
    nc = bacc.Bacc("TRN2", target_bir_lowering=False, num_devices=1)
    args = [nc.dram_tensor(f"in_{k}", a.shape, mybir.dt.from_np(a.dtype), kind="ExternalInput").ap()
            for k, a in arrays.items()]
    means = nc.dram_tensor("means", [P, NT], F32, kind="Internal").ap()
    out = nc.dram_tensor("out", x.shape, F32, kind="ExternalOutput").ap()
    build(nc, *args, means, out)
    r = run_bass_kernel_spmd(nc, [{f"in_{k}": a for k, a in arrays.items()}], core_ids=[0])
    return r.results[0]["out"]
```
